# Optimizing a Trainium2 kernel written in Bass

```python
import numpy as np
import jax
import jax.numpy as jnp

def _softmax(x, axis=-1):
    return jax.nn.softmax(x, axis=axis)
def _gelu(x):
    return jax.nn.gelu(x, approximate=True)
def _silu(x):
    return jax.nn.silu(x)
def _sigmoid(x):
    return jax.nn.sigmoid(x)
def _layernorm(x, axis=-1, eps=1e-5):
    m = jnp.mean(x, axis=axis, keepdims=True)
    v = jnp.var(x, axis=axis, keepdims=True)
    return (x - m) / jnp.sqrt(v + eps)
def _scatter_add(tgt, idx, src, axis=0):
    return tgt.at[idx].add(src)
def _segment_sum(src, seg, n):
    return jax.ops.segment_sum(src, seg, n)

kernel_name = 'mk_conv_preact_d2_conv_nchw64_e97c25'

def setup_inputs(seed: int = 0):
    np.random.seed(seed)
    _w = jnp.asarray
    def _rec_inputs():
        import jax
        import jax.numpy as jnp
        _gk = jax.random.key(seed)
        x = -0.000125 + 0.9999 * jax.random.normal(jax.random.fold_in(_gk, 1), (8, 64, 256, 256), jnp.float32)
        return x
    x = _rec_inputs()
    def _L0_conv_setup():
        import jax, jax.numpy as jnp
        import numpy as np
        MODES1 = 32
        MODES2 = 32

        def _dct1_last(x):
            ext = jnp.concatenate([x, x[..., -2:0:-1]], axis=-1)
            return jnp.fft.rfft(ext, axis=-1).real.astype(x.dtype)

        def _dct1_2d(x):
            x = _dct1_last(x)
            x = jnp.swapaxes(x, -1, -2)
            x = _dct1_last(x)
            return jnp.swapaxes(x, -1, -2)
        key = jax.random.key(seed)
        k1, k2, k3 = jax.random.split(key, 3)
        B, Cin, Cout, H, W = (8, 64, 64, 256, 256)
        scale = 1.0 / (Cin * Cout)
        x = jax.random.normal(k1, (B, Cin, H, W), dtype=jnp.float32)
        weights1 = scale * jax.random.uniform(k2, (Cin, Cout, MODES1, MODES2), dtype=jnp.float32)
        weights2 = scale * jax.random.uniform(k3, (Cin, Cout, MODES1, MODES2), dtype=jnp.float32)
        return {'x': x, 'weights1': weights1, 'weights2': weights2}
    _L0_conv_all = _L0_conv_setup()
    _L0_conv_in = {k: v for k, v in _L0_conv_all.items() if k in ('weights1', 'weights2', )}
    del _L0_conv_all

    def _L1_conv_setup():
        import jax, jax.numpy as jnp
        import numpy as np
        key = jax.random.key(seed)
        k1, k2 = jax.random.split(key)
        B, H, W, D, K = (32, 64, 64, 64, 1024)
        x = jax.random.normal(k1, (B, H, W, D), dtype=jnp.float32)
        embeddings = jax.random.normal(k2, (D, K), dtype=jnp.float32) * 0.1
        return {'x': x, 'embeddings': embeddings}
    _L1_conv_all = _L1_conv_setup()
    _L1_conv_in = {k: v for k, v in _L1_conv_all.items() if k in ('embeddings', )}
    del _L1_conv_all

    return {
        "x": x,
        "L0_conv_weights1": _L0_conv_in["weights1"],
        "L0_conv_weights2": _L0_conv_in["weights2"],
        "L1_conv_embeddings": _L1_conv_in["embeddings"],
    }

def reference(x, L0_conv_weights1, L0_conv_weights2, L1_conv_embeddings):
    import jax
    import jax.numpy as jnp
    def _L0_conv_ref(x, weights1, weights2):
        import jax, jax.numpy as jnp
        import numpy as np
        MODES1 = 32
        MODES2 = 32

        def _dct1_last(x):
            ext = jnp.concatenate([x, x[..., -2:0:-1]], axis=-1)
            return jnp.fft.rfft(ext, axis=-1).real.astype(x.dtype)

        def _dct1_2d(x):
            x = _dct1_last(x)
            x = jnp.swapaxes(x, -1, -2)
            x = _dct1_last(x)
            return jnp.swapaxes(x, -1, -2)
        B, Cin, H, W = x.shape
        Cout = weights1.shape[1]
        Wh = W // 2 + 1
        m1, m2 = (MODES1, MODES2)
        x_dct = _dct1_2d(x)
        low = jnp.einsum('bixy,ioxy->boxy', x_dct[:, :, :m1, :m2], weights1)
        high = jnp.einsum('bixy,ioxy->boxy', x_dct[:, :, -m1:, :m2], weights2)
        out_ft = jnp.zeros((B, Cout, H, Wh), dtype=x.dtype)
        out_ft = out_ft.at[:, :, :m1, :m2].set(low)
        out_ft = out_ft.at[:, :, H - m1:, :m2].set(high)
        out_full = jnp.pad(out_ft, ((0, 0), (0, 0), (0, 0), (0, W - Wh)))
        return _dct1_2d(out_full)

    def _L1_conv_ref(x, embeddings):
        import jax, jax.numpy as jnp
        import numpy as np
        input_shape = x.shape
        D = embeddings.shape[0]
        flat = x.reshape(-1, D)
        y_sq = jnp.sum(flat * flat, axis=1, keepdims=True)
        e_sq = jnp.sum(embeddings * embeddings, axis=0)
        sim = jnp.einsum('nd,dk->nk', flat, embeddings)
        distances = y_sq + e_sq - 2.0 * sim
        codes = jnp.argmin(distances, axis=1)
        quantized = jnp.take(embeddings.T, codes, axis=0)
        return quantized.reshape(input_shape)

    def _gn(v, G=32, eps=1e-5):
        B_, C_, H_, W_ = v.shape
        g = v.reshape(B_, G, C_ // G, H_, W_)
        m = jnp.mean(g, axis=(2, 3, 4), keepdims=True)
        s = jnp.var(g, axis=(2, 3, 4), keepdims=True)
        return ((g - m) / jnp.sqrt(s + eps)).reshape(v.shape)

    def _ln_c(v, eps=1e-6):
        m = jnp.mean(v, axis=1, keepdims=True)
        s = jnp.var(v, axis=1, keepdims=True)
        return (v - m) / jnp.sqrt(s + eps)

    def _ln_t(v, eps=1e-5):
        m = jnp.mean(v, axis=-1, keepdims=True)
        s = jnp.var(v, axis=-1, keepdims=True)
        return (v - m) / jnp.sqrt(s + eps)

    def _to_tokens(v):
        B_, C_, H_, W_ = v.shape
        return v.reshape(B_, C_, H_ * W_).transpose(0, 2, 1)
    def _from_tokens(t, like):
        B_, C_, H_, W_ = like.shape
        return t.transpose(0, 2, 1).reshape(B_, C_, H_, W_)

    x = x + _L0_conv_ref(_gn(x), L0_conv_weights1, L0_conv_weights2)
    x = x + _L1_conv_ref(_gn(x), L1_conv_embeddings)
    return x


_drawn_inputs = setup_inputs


def setup_inputs(seed=0):
    import zlib

    import numpy as np

    out = dict(_drawn_inputs(seed))
    spreads = {}
    factors = {'L1_conv_embeddings': 35.263}
    for name, (base, spread) in spreads.items():
        noise = np.random.default_rng([zlib.crc32(name.encode()), seed]).standard_normal(out[name].shape)
        drawn = base * np.exp(spread * noise) if base else spread * noise
        out[name] = jnp.asarray(drawn.astype(out[name].dtype))
    for name, factor in factors.items():
        out[name] = (out[name] * factor).astype(out[name].dtype)
    return out
```

```python
from contextlib import ExitStack

import numpy as np

import concourse.bass as bass
from concourse import mybir

ALU = mybir.AluOpType
ACT = mybir.ActivationFunctionType
AX_X = mybir.AxisListType.X
F32 = mybir.dt.float32
F16 = mybir.dt.float16
I32 = mybir.dt.int32
U32 = mybir.dt.uint32
RMAX = bass.bass_isa.ReduceOp.max

P = 128
B, C, H, W = 8, 64, 256, 256
CG = 2
NG = B * C // CG
U = 4
NI = NG // U
T2 = H // P
MX, MY = 64, 32
HALF = MX // 2 * MY
CH = 64
NCH = HALF // CH
D = 64
K = 1024
NP = K // 2
NT = CG * H * W // D // P
ROW = 3 * D + 4
DC = float((2 * (H - 1)) * (2 * (W - 1)))
EPS = 1e-5
E_SCALE = 2.0 ** 14
Y_SCALE = 2.0 ** 7
ONE = 2.0 ** 15


class Group:

    def __init__(self, i, r):
        self.i, self.r = i + r // U if isinstance(i, int) else i, r % U if isinstance(i, int) else r
        self.n = U * self.i + self.r
        self.buf4 = r % 4
        self.buf2 = r % 2
        self.quarter = self.i + self.r // 4 if not isinstance(i, int) else self.n // 4
        self.half = 2 * self.i + self.r // 2 if not isinstance(i, int) else self.n // 2

    def exists(self):
        return not isinstance(self.n, int) or 0 <= self.n < NG


def need(eng, sem, count):
    if not isinstance(count, int) or count > 0:
        eng.wait_ge(sem, count)


def program(nc, x, w1, w2, emb, c_fh, c_fw, c_ih, c_iw, c_id, c_gm, c_rm, out):
    spec = nc.dram_tensor("spec", [B, C, MX * MY], F32, kind="Internal").ap()
    mixed = nc.dram_tensor("mixed", [B, C, MX * MY], F32, kind="Internal").ap()
    table = nc.dram_tensor("table", [NP, ROW], F32, kind="Internal").ap()

    x_g = x.rearrange("b (g i) (p t) w -> (b g) p i (t w)", i=CG, t=T2)
    out_g = out.rearrange("b (g i) (p t) w -> (b g) p i (t w)", i=CG, t=T2)
    spec_g = spec.rearrange("b (g i) (x y) -> (b g) (i x) y", i=CG, y=MY)
    spec_c = spec.rearrange("b c m -> c b m")
    mixed_c = mixed.rearrange("b o m -> o b m")
    mixed_g = mixed.rearrange("b (g i) (x y) -> (b g) x i y", i=CG, y=MY)
    w_m = [w.rearrange("i o x y -> i o (x y)") for w in (w1, w2)]

    with ExitStack() as ctx:
        def sb(name, shape, dt=F32):
            return ctx.enter_context(nc.sbuf_tensor(name, shape, dt))

        def sem(name):
            return ctx.enter_context(nc.semaphore(name))

        bank = [ctx.enter_context(nc.psum_tensor(f"bank{n}", [P, 512], F32)) for n in range(8)]

        fh = sb("fh", [P, T2, MX])
        fw = sb("fw", [P, 2, MY])
        ih = sb("ih", [MX, T2 * P])
        iw = sb("iw", [CG * MY, W])
        ident = sb("ident", [P, P])
        gmask = sb("gmask", [P, C // CG])
        rmask = sb("rmask", [P, 3])
        ident16 = sb("ident16", [P, P], F16)
        avg = sb("avg", [P, P])
        ones = sb("ones", [D, P])
        mhalf = sb("mhalf", [P, NG])
        consts = ((fh, c_fh), (fw, c_fw), (ih, c_ih), (iw, c_iw), (ident, c_id), (gmask, c_gm), (rmask, c_rm))

        E = sb("E", [P, NP, 2])
        S = sb("S", [P, 2, NP])
        S2 = sb("S2", [P, 2, NP])
        eh = sb("eh", [P, 2, NP], F16)
        el = sb("el", [P, 2, NP], F16)
        part = sb("part", [P, 2, NP], F16)
        tb = sb("tb", [P, 4, ROW])
        tsq = sb("tsq", [P, 4, 2, D])
        tnorm = sb("tnorm", [P, 4, 2])
        sc = sb("sc", [P, 8])
        amax0, amax, inv_a, inv_s, ymul, ymulh, bscale, escale = (sc[:, n:n + 1] for n in range(8))

        X = sb("X", [P, 4, CG * T2 * W])
        st = sb("st", [P, U, 2, 6])
        mvs = sb("mvs", [P, U, 2])
        mv_all = sb("mv_all", [P, NG, 2])
        dev_all = sb("dev_all", [P, NG])
        var_all = sb("var_all", [P, NG])
        rstd_all = sb("rstd_all", [P, NG])
        mean_all = sb("mean_all", [P, NG])
        sel8 = sb("sel8", [P, B, C // CG])
        r_c = sb("r_c", [P, B])
        m_c = sb("m_c", [P, B])
        dc_fix = sb("dc_fix", [P, NCH * B])
        Us = sb("Us", [MX, 2, 512])
        UTs = sb("UTs", [P, 2, 256])
        Fs = sb("Fs", [P, U, MY])
        Wc = sb("Wc", [P, 2, C, CH])
        Xc = sb("Xc", [P, 2, B, CH])
        Oc = sb("Oc", [P, 2, B, CH])
        M = sb("M", [MX, 2, CG * MY])
        Ts = sb("Ts", [CG * MY, T2 * P])
        bst = sb("bst", [P, 2, 6])
        mv = sb("mv", [P, 2])
        small = sb("small", [P, 8])
        dev, wv, ve, negm, rs, rr, nb = (small[:, n:n + 1] for n in range(7))
        YS = sb("YS", [P, NT, 2 * D], F16)
        Y = sb("Y", [P, 2, NT, D])
        t1 = sb("t1", [P, 2, NT, P], F16)
        t2 = sb("t2", [P, 2, NT, P], F16)
        R = sb("R", [P, 2, NP])
        Fm = sb("Fm", [P, 4, NP])
        mx = sb("mx", [P, 4])
        idx = sb("idx", [P, 2, NT, 8], U32)
        q = sb("q", [P, 2, NT, ROW])
        prod = sb("prod", [P, NT, D])
        dot = sb("dot", [P, NT])
        odd = sb("odd", [P, NT], I32)

        consts_in = sem("consts_in")
        emb_in = sem("emb_in")
        held = {n: sem(f"held_{n}") for n in ("pe", "act", "dve", "pool")}
        dve_step = sem("dve_step")
        ids_ready = sem("ids_ready")
        amax_in = sem("amax_in")
        amax_all = sem("amax_all")
        esq_in = sem("esq_in")
        esq_done = sem("esq_done")
        tab_tr = sem("tab_tr")
        tab_ready = sem("tab_ready")
        tab_out = sem("tab_out")
        codes_ready = sem("codes_ready")

        xa_in = [sem(f"xa_in{n}") for n in range(U)]
        a_h, a_u, a_tr, a_ut, a_w, a_f = (sem(n) for n in ("a_h", "a_u", "a_tr", "a_ut", "a_w", "a_f"))
        a_bn, a_mv, a_mvc = (sem(n) for n in ("a_bn", "a_mv", "a_mvc"))
        fs_out = [sem(f"fs_out{n}") for n in range(U)]
        s_mean, s_dev, s_var, s_ve, s_rstd = (sem(n) for n in ("s_mean", "s_dev", "s_var", "s_ve", "s_rstd"))
        w_in = [sem(f"w_in{n}") for n in range(2)]
        xs_in = [sem(f"xs_in{n}") for n in range(2)]
        m_sc, m_x, m_mm, m_ev = (sem(n) for n in ("m_sc", "m_x", "m_mm", "m_ev"))
        o_out = [sem(f"o_out{n}") for n in range(2)]

        x_in = [sem(f"x_in{n}") for n in range(4)]
        m_in = [sem(f"m_in{n}") for n in range(2)]
        y_out = [sem(f"y_out{n}") for n in range(4)]
        gath = [sem(f"gath{n}") for n in range(4)]
        b_inv, b_t, b_conv, b_x1, b_bn, b_mv, b_st1, b_dev, b_w, b_st2, b_ve, b_rs, b_rr, b_nb = (
            sem("b_" + n) for n in "inv t conv x1 bn mv st1 dev w st2 ve rs rr nb".split())
        b_y, b_yl, b_tp, b_te, b_sc, b_rl, b_ttr, b_mi, b_p, b_red, b_sel, b_pr, b_fin = (
            sem("b_" + n) for n in "y yl tp te sc rl ttr mi p red sel pr fin".split())

        def hold(eng, name, count):
            if not isinstance(count, int):
                eng.sem_inc(held[name], 1)

        block = ctx.enter_context(nc.Block())

        @block.sync
        def _(sp):
            sp.dma_start(E[0:D], emb.rearrange("d (j e) -> d j e", e=2)).then_inc(emb_in, 16)
            sp.dma_start(E[D:P], emb.rearrange("d (j e) -> d j e", e=2)).then_inc(emb_in, 16)
            for tile, src in consts:
                sp.dma_start(tile[:], src).then_inc(consts_in, 16)

            def load_weights(c, v):
                for n in range(2):
                    sp.dma_start(Wc[64 * n:64 * n + 64, v], w_m[n][:, :, bass.ds(c * CH, CH)]).then_inc(w_in[v], 16)

            def group_a(g):
                need(sp, a_h, g.n - 3)
                need(sp, a_bn, g.n - 3)
                sp.dma_start(X[:, g.buf4].rearrange("p (i f) -> p i f", i=CG), x_g[g.n]).then_inc(xa_in[g.buf4], 16)

            def store_a(g):
                need(sp, a_f, g.n + 1)
                sp.dma_start(spec_g[g.n], Fs[:, g.buf4]).then_inc(fs_out[g.buf4], 16)

            for r in range(U):
                group_a(Group(0, r))
            load_weights(0, 0)
            load_weights(1, 1)
            with sp.Fori(1, NI) as i:
                for r in range(U):
                    store_a(Group(i, r - U))
                    group_a(Group(i, r))
            for r in range(U):
                store_a(Group(NI - 1, r))
            sp.wait_ge(tab_ready, 1)
            sp.dma_start(table.rearrange("(c p) w -> p c w", p=P), tb[:]).then_inc(tab_out, 16)
            for n in range(U):
                sp.wait_ge(fs_out[n], 16 * NI)

            def load_m(i, v):
                c = 2 * i + v
                need(sp, m_mm, c - 1)
                for n in range(2):
                    sp.dma_start(Xc[64 * n:64 * n + 64, v],
                                 spec_c[:, :, bass.ds(c * CH + n * HALF, CH)]).then_inc(xs_in[v], 16)
                if not (isinstance(i, int) and i == 0):
                    load_weights(c, v)

            load_m(0, 0)
            load_m(0, 1)
            with sp.Fori(1, NCH // 2) as i:
                for v in range(2):
                    load_m(i, v)

            def load_x(g):
                need(sp, y_out[g.buf4], 16 * g.quarter)
                sp.dma_start(X[:, g.buf4].rearrange("p (i f) -> p i f", i=CG), x_g[g.n]).then_inc(x_in[g.buf4], 16)

            def load_modes(g):
                need(sp, b_inv, g.n - 1)
                sp.dma_start(M[:, g.buf2].rearrange("p (i y) -> p i y", i=CG), mixed_g[g.n]).then_inc(m_in[g.buf2], 16)

            def store_y(g):
                need(sp, b_fin, g.n + 1)
                sp.dma_start(out_g[g.n], X[:, g.buf4].rearrange("p (i f) -> p i f", i=CG)).then_inc(y_out[g.buf4], 16)

            sp.wait_ge(a_h, NG)
            sp.wait_ge(a_bn, NG)
            for r in range(3):
                load_x(Group(0, r))
            for n in range(2):
                sp.wait_ge(o_out[n], 32 * (NCH // 2))
            for r in range(2):
                load_modes(Group(0, r))

            def body(i):
                for r in range(U):
                    if Group(i, r + 2).exists():
                        load_modes(Group(i, r + 2))
                    if Group(i, r - 1).exists():
                        store_y(Group(i, r - 1))
                    if Group(i, r + 3).exists():
                        load_x(Group(i, r + 3))

            body(0)
            with sp.Fori(1, NI - 1) as i:
                body(i)
            body(NI - 1)
            store_y(Group(NI - 1, U - 1))
            for n in range(4):
                sp.wait_ge(y_out[n], 16 * NI)

        @block.tensor
        def _(pe):
            pe.wait_ge(consts_in, 16 * len(consts))
            pe.wait_ge(ids_ready, 1)

            pe.wait_ge(esq_in, 1)
            for e in range(2):
                last = nc.tensor.matmul(bank[e][:], ones[:], S2[0:D, e], start=True, stop=True)
            last.then_inc(esq_done, 1)
            for c in range(4):
                for e in range(2):
                    last = nc.tensor.transpose(bank[2][:, (2 * c + e) * D:(2 * c + e + 1) * D],
                                               E[0:D, c * P:(c + 1) * P, e], ident[0:D, 0:D])
            last.then_inc(tab_tr, 1)
            pe.wait_ge(codes_ready, 1)

            def dct_h(g):
                need(pe, xa_in[g.buf4], 16 * (g.quarter + 1))
                need(pe, a_u, g.n - 1)
                xg = X[:, g.buf4].rearrange("p (i t w) -> p t i w", i=CG, t=T2)
                for t in range(T2):
                    last = nc.tensor.matmul(bank[g.buf2][0:MX], fh[:, t], xg[:, t], start=t == 0, stop=t == T2 - 1)
                last.then_inc(a_h, 1)

            def turn(g):
                need(pe, a_u, g.n + 1)
                need(pe, a_ut, g.n - 1)
                hold(pe, "pe", g.n)
                for wc in range(2):
                    for i in range(CG):
                        last = nc.tensor.transpose(bank[2 + g.buf2][:, (2 * wc + i) * MX:(2 * wc + i + 1) * MX],
                                                   Us[:, g.buf2, i * W + wc * P:i * W + (wc + 1) * P],
                                                   ident[0:MX, 0:MX])
                last.then_inc(a_tr, 1)

            def dct_w(g):
                need(pe, a_ut, g.n + 1)
                need(pe, a_f, g.n - 1)
                for wc in range(2):
                    last = nc.tensor.matmul(bank[4 + g.buf2][:, 0:MY], UTs[:, g.buf2, wc * P:(wc + 1) * P],
                                            fw[:, wc], start=wc == 0, stop=wc == 1)
                last.then_inc(a_w, 1)

            def body_a(i):
                for r in range(U):
                    dct_h(Group(i, r))
                    if Group(i, r - 2).exists():
                        dct_w(Group(i, r - 2))
                    if Group(i, r - 1).exists():
                        turn(Group(i, r - 1))

            body_a(0)
            with pe.Fori(1, NI) as i:
                body_a(i)
            dct_w(Group(NI - 1, U - 2))
            turn(Group(NI - 1, U - 1))
            dct_w(Group(NI - 1, U - 1))

            pe.wait_ge(a_mvc, NI)
            nc.tensor.matmul(bank[6][:, 0:NG], avg[:], mv_all[:, :, 0], start=True, stop=True).then_inc(s_mean, 1)
            pe.wait_ge(s_dev, 1)
            nc.tensor.matmul(bank[7][:, 0:NG], avg[:], dev_all[:], start=True, stop=True).then_inc(s_var, 1)

            pe.wait_ge(a_ut, NG)
            pe.wait_ge(a_f, NG)

            def mix(i, v):
                c = 2 * i + v
                need(pe, w_in[v], 32 * (i + 1))
                need(pe, m_x, c + 1)
                need(pe, m_ev, c - 1)
                hold(pe, "pe", i)
                for m in range(CH):
                    for n in range(2):
                        half = slice(64 * n, 64 * n + 64)
                        last = nc.tensor.matmul(bank[2 * v + n][half, m * B:(m + 1) * B], Wc[half, v, :, m],
                                                Xc[half, v, :, m], start=True, stop=True)
                last.then_inc(m_mm, 1)

            mix(0, 0)
            mix(0, 1)
            with pe.Fori(1, NCH // 2) as i:
                for v in range(2):
                    mix(i, v)

            pe.wait_ge(m_ev, NCH)
            pe.wait_ge(s_ve, 1)
            tp = bank[7][:].bitcast(F16).rearrange("p (k f) -> p k f", k=NT // 2)

            def inverse_h(g):
                need(pe, m_in[g.buf2], 16 * (g.half + 1))
                need(pe, b_ve, g.n)
                hold(pe, "pe", g.n)
                nc.tensor.matmul(bank[6][0:CG * MY, 0:T2 * P], M[:, g.buf2], ih[:], start=True,
                                 stop=True).then_inc(b_inv, 1)

            def inverse_w(g):
                need(pe, b_t, g.n + 1)
                need(pe, b_x1, g.n)
                for t in range(T2):
                    for i in range(CG):
                        rows = slice(i * MY, (i + 1) * MY)
                        last = nc.tensor.matmul(bank[4 + i][:, t * W:(t + 1) * W], Ts[rows, t * P:(t + 1) * P],
                                                iw[rows], start=True, stop=True)
                last.then_inc(b_conv, 1)

            def mean(g):
                need(pe, b_mv, g.n + 1)
                nc.tensor.matmul(bank[6][:, 256:257], avg[:], mv[:, 0:1], start=True, stop=True).then_inc(b_st1, 1)

            def variance(g):
                need(pe, b_w, g.n + 1)
                nc.tensor.matmul(bank[6][:, 257:258], avg[:], wv, start=True, stop=True).then_inc(b_st2, 1)

            def turn_y(g, half):
                need(pe, b_yl, g.n + 1)
                need(pe, b_te, 2 * g.n + half)
                for k in range(NT // 2):
                    last = nc.tensor.transpose(tp[:, k], YS[:, half * (NT // 2) + k], ident16[:])
                last.then_inc(b_tp, 1)

            def scores(g, k):
                n = NT * g.n + k
                if k % (NT // 2) == 0:
                    need(pe, b_te, 2 * g.n + 1 + k // (NT // 2))
                need(pe, b_ttr, n - 1)
                for rows, tile, codes in ((P, t1, eh), (D + 3, t2, el)):
                    for e in range(2):
                        last = nc.tensor.matmul(bank[2 * (k % 2) + e][:], tile[0:rows, g.buf2, k],
                                                codes[0:rows, e], start=rows == P, stop=rows != P)
                last.then_inc(b_sc, 1)

            def prepare(g):
                inverse_h(g)
                inverse_w(g)
                mean(g)
                variance(g)
                turn_y(g, 0)

            def body_b(i):
                for r in range(U):
                    g, after = Group(i, r), Group(i, r + 1)
                    for k in range(NT):
                        scores(g, k)
                        if k == 1:
                            turn_y(g, 1)
                        if after.exists():
                            if k == 0:
                                inverse_h(after)
                            if k == 2:
                                inverse_w(after)
                            if k == 4:
                                mean(after)
                            if k == 6:
                                variance(after)
                            if k == 13:
                                turn_y(after, 0)

            prepare(Group(0, 0))
            body_b(0)
            with pe.Fori(1, NI - 1) as i:
                body_b(i)
            body_b(NI - 1)

        @block.scalar
        def _(act):
            def take_u(g):
                need(act, a_h, g.n + 1)
                need(act, a_tr, g.n - 1)
                nc.scalar.copy(Us[:, g.buf2], bank[g.buf2][0:MX]).then_inc(a_u, 1)

            def take_f(g):
                need(act, a_w, g.n + 1)
                need(act, fs_out[g.buf4], 16 * g.quarter)
                nc.scalar.copy(Fs[:, g.buf4], bank[4 + g.buf2][:, 0:MY]).then_inc(a_f, 1)

            def body_a(i):
                for r in range(U):
                    take_u(Group(i, r))
                    if Group(i, r - 2).exists():
                        take_f(Group(i, r - 2))

            body_a(0)
            with act.Fori(1, NI) as i:
                body_a(i)
            take_f(Group(NI - 1, U - 2))
            take_f(Group(NI - 1, U - 1))

            def take_mix(i, v):
                c = 2 * i + v
                need(act, m_mm, c + 1)
                need(act, o_out[v], 32 * i)
                for n in range(2):
                    half = slice(64 * n, 64 * n + 64)
                    last = nc.scalar.copy(Oc[half, v].rearrange("p b m -> p m b"),
                                          bank[2 * v + n][half].rearrange("p (m b) -> p m b", b=B))
                last.then_inc(m_ev, 1)
                act.wait_ge(m_ev, c + 1)
                for n in range(2):
                    act.dma_start(mixed_c[:, :, bass.ds(c * CH + n * HALF, CH)],
                                  Oc[64 * n:64 * n + 64, v]).then_inc(o_out[v], 16)

            take_mix(0, 0)
            take_mix(0, 1)
            with act.Fori(1, NCH // 2) as i:
                for v in range(2):
                    take_mix(i, v)

            tp = bank[7][:].bitcast(F16).rearrange("p (k f) -> p k f", k=NT // 2)

            def take_t(g):
                need(act, b_inv, g.n + 1)
                need(act, b_conv, g.n)
                nc.scalar.copy(Ts[:], bank[6][0:CG * MY, 0:T2 * P]).then_inc(b_t, 1)

            def normalise(g):
                need(act, b_nb, g.n + 1)
                need(act, b_tp, 2 * g.n)
                need(act, b_p, g.n - 1)
                xg = X[:, g.buf4].rearrange("p (k d) -> p k d", d=D)
                nc.scalar.activation(YS[:, :, 0:D], xg, ACT.Identity, bias=nb, scale=rr)
                nc.scalar.activation(Y[:, g.buf2], xg, ACT.Identity, bias=nb, scale=rr).then_inc(b_y, 1)

            def take_y(g, half):
                need(act, b_tp, 2 * g.n + half + 1)
                need(act, b_sc, NT * (g.n - 1))
                ks = slice(half * (NT // 2), (half + 1) * (NT // 2))
                nc.scalar.copy(t1[:, g.buf2, ks], tp)
                nc.scalar.copy(t2[0:D, g.buf2, ks], tp[0:D]).then_inc(b_te, 1)

            def relu(g, k):
                n = NT * g.n + k
                need(act, b_sc, n + 1)
                need(act, b_ttr, n - 1)
                nc.scalar.activation(R[:, k % 2], bank[2 * (k % 2) + 1][:], ACT.Relu).then_inc(b_rl, 1)

            def prepare(g):
                take_t(g)
                normalise(g)
                take_y(g, 0)

            def body_b(i):
                for r in range(U):
                    g, after = Group(i, r), Group(i, r + 1)
                    for k in range(NT):
                        relu(g, k)
                        if k == 2:
                            take_y(g, 1)
                        if after.exists():
                            if k == 0:
                                take_t(after)
                            if k == 8:
                                normalise(after)
                            if k == 14:
                                take_y(after, 0)

            act.wait_ge(codes_ready, 1)
            prepare(Group(0, 0))
            body_b(0)
            with act.Fori(1, NI - 1) as i:
                body_b(i)
            body_b(NI - 1)

        @block.vector
        def _(dve):
            steps = [0]

            def then(ins):
                steps[0] += 1
                ins.then_inc(dve_step, 1)
                dve.wait_ge(dve_step, steps[0])

            V = nc.vector
            V.memset(avg[:], 1.0 / P)
            V.memset(ones[:], 1.0)
            V.memset(mhalf[:], -0.5)
            V.memset(t2[D:P], ONE)
            V.memset(dc_fix[:], 0.0)
            V.memset(tb[:], 0.0)
            dve.wait_ge(consts_in, 16 * len(consts))
            V.tensor_copy(ident16[:], ident[:]).then_inc(ids_ready, 1)

            dve.wait_ge(emb_in, 32)
            Ef = E[:].rearrange("p j e -> p (j e)")
            V.tensor_reduce(amax0, Ef, AX_X, ALU.max, apply_absolute_value=True).then_inc(amax_in, 1)
            V.tensor_tensor(S2[:].rearrange("p e j -> p j e"), E[:], E[:], ALU.mult).then_inc(esq_in, 1)
            dve.wait_ge(amax_all, 1)
            then(V.tensor_scalar(amax, amax, 1e-30, None, ALU.max))
            then(V.reciprocal(inv_a, amax))
            then(V.tensor_scalar(inv_s, amax, 1.0 / 16.0, 1.0, ALU.mult, ALU.max))
            then(V.reciprocal(inv_s, inv_s))
            V.tensor_scalar(ymul, inv_s, Y_SCALE, None, ALU.mult)
            V.tensor_scalar(ymulh, inv_s, Y_SCALE / 2, None, ALU.mult)
            V.tensor_scalar(escale, inv_a, E_SCALE, None, ALU.mult)
            then(V.scalar_tensor_tensor(bscale, inv_a, -Y_SCALE * E_SCALE / 2 / ONE, inv_s, ALU.mult, ALU.mult))
            then(V.tensor_tensor(S[:, 1], E[:, :, 1], E[:, :, 0], ALU.subtract))
            V.tensor_scalar(S[:, 0], E[:, :, 0], escale, None, ALU.mult)
            then(V.tensor_scalar(S[:, 1], S[:, 1], escale, None, ALU.mult))
            then(V.tensor_copy(eh[:], S[:]))
            then(V.tensor_tensor(el[0:D], S[0:D], eh[0:D], ALU.subtract))
            dve.wait_ge(esq_done, 1)
            then(V.tensor_copy(S[:, 0], bank[0][:]))
            then(V.tensor_tensor(S[:, 1], bank[1][:], S[:, 0], ALU.subtract))
            then(V.tensor_scalar(S[:], S[:], bscale, None, ALU.mult))
            for n in range(3):
                then(V.tensor_copy(part[:], S[:]))
                if n == 0:
                    then(V.tensor_scalar(el[D:P], part[D:P], rmask[D:P, 0:1], None, ALU.mult))
                else:
                    then(V.scalar_tensor_tensor(el[D:P], part[D:P], rmask[D:P, n:n + 1], el[D:P], ALU.mult, ALU.add))
                if n < 2:
                    then(V.tensor_tensor(S[:], S[:], part[:], ALU.subtract))
            dve.wait_ge(tab_tr, 1)
            tt = bank[2][:].rearrange("p (c e d) -> p c e d", c=4, e=2)
            V.tensor_copy(tb[:, :, 0:D], tt[:, :, 0])
            then(V.tensor_copy(tb[:, :, D:2 * D], tt[:, :, 1]))
            V.tensor_tensor(tb[:, :, 2 * D:3 * D], tb[:, :, D:2 * D], tb[:, :, 0:D], ALU.subtract)
            te = tb[:, :, 0:2 * D].rearrange("p c (e d) -> p c e d", e=2)
            then(V.tensor_tensor(tsq[:], te, te, ALU.mult))
            then(V.tensor_reduce(tnorm[:], tsq[:], AX_X, ALU.add))
            then(V.tensor_tensor(tnorm[:, :, 0], tnorm[:, :, 1], tnorm[:, :, 0], ALU.subtract))
            then(V.tensor_scalar(tb[:, :, 3 * D], tnorm[:, :, 0], ymulh, None, ALU.mult))
            dve.sem_inc(tab_ready, 1)
            dve.sem_inc(codes_ready, 2)

            def stats(g):
                need(dve, xa_in[g.buf4], 16 * (g.quarter + 1))
                for n in range(2):
                    last = V.bn_stats(st[:, g.buf4, n], X[:, g.buf4, 512 * n:512 * (n + 1)])
                last.then_inc(a_bn, 1)

            def join(g):
                need(dve, a_bn, g.n + 1)
                need(dve, a_mvc, g.quarter)
                hold(dve, "dve", g.n)
                V.bn_aggr(mvs[:, g.buf4], st[:, g.buf4]).then_inc(a_mv, 1)

            def take_ut(g):
                need(dve, a_tr, g.n + 1)
                need(dve, a_w, g.n - 1)
                V.tensor_copy(UTs[:, g.buf2], bank[2 + g.buf2][:, 0:256]).then_inc(a_ut, 1)

            def body_a(i):
                for r in range(U):
                    stats(Group(i, r))
                    if Group(i, r - 1).exists():
                        take_ut(Group(i, r - 1))
                    join(Group(i, r))
                need(dve, a_mv, U * (i + 1))
                V.tensor_copy(mv_all[:, bass.ds(U * i, U), :], mvs[:]).then_inc(a_mvc, 1)

            body_a(0)
            with dve.Fori(1, NI) as i:
                body_a(i)
            take_ut(Group(NI - 1, U - 1))

            dve.wait_ge(s_mean, 1)
            then(V.tensor_copy(mean_all[:], bank[6][:, 0:NG]))
            then(V.tensor_tensor(dev_all[:], mv_all[:, :, 0], mean_all[:], ALU.subtract))
            then(V.tensor_tensor(dev_all[:], dev_all[:], dev_all[:], ALU.mult))
            V.tensor_tensor(dev_all[:], dev_all[:], mv_all[:, :, 1], ALU.add).then_inc(s_dev, 1)
            dve.wait_ge(s_var, 1)
            V.tensor_scalar(var_all[:], bank[7][:, 0:NG], EPS, None, ALU.add).then_inc(s_ve, 1)
            dve.wait_ge(s_rstd, 1)
            gm = gmask[:].unsqueeze(1).broadcast_to([P, B, C // CG])
            then(V.tensor_tensor(sel8[:], rstd_all[:].rearrange("p (b g) -> p b g", b=B), gm, ALU.mult))
            then(V.tensor_reduce(r_c[:], sel8[:], AX_X, ALU.add))
            then(V.tensor_tensor(sel8[:], mean_all[:].rearrange("p (b g) -> p b g", b=B), gm, ALU.mult))
            then(V.tensor_reduce(m_c[:], sel8[:], AX_X, ALU.add))
            then(V.scalar_tensor_tensor(dc_fix[0:C, 0:B], m_c[0:C], DC, r_c[0:C], ALU.mult, ALU.mult))

            def scale(i, v):
                c = 2 * i + v
                need(dve, xs_in[v], 32 * (i + 1))
                V.tensor_tensor(Xc[:, v], Xc[:, v], r_c[:].unsqueeze(2).broadcast_to([P, B, CH]),
                                ALU.mult).then_inc(m_sc, 1)
                dve.wait_ge(m_sc, c + 1)
                V.tensor_tensor(Xc[:, v, :, 0], Xc[:, v, :, 0], dc_fix[:, bass.ds(c * B, B)],
                                ALU.subtract).then_inc(m_x, 1)

            scale(0, 0)
            scale(0, 1)
            with dve.Fori(1, NCH // 2) as i:
                for v in range(2):
                    scale(i, v)

            def residual(g):
                need(dve, b_conv, g.n + 1)
                need(dve, x_in[g.buf4], 16 * (g.quarter + 1))
                for n in range(2):
                    xg = X[:, g.buf4, 512 * n:512 * (n + 1)]
                    last = V.tensor_tensor(xg, bank[4 + n][:], xg, ALU.add)
                last.then_inc(b_x1, 1)
                need(dve, b_x1, g.n + 1)
                for n in range(2):
                    last = V.bn_stats(bst[:, n], X[:, g.buf4, 512 * n:512 * (n + 1)])
                last.then_inc(b_bn, 1)
                need(dve, b_bn, g.n + 1)
                hold(dve, "dve", g.n)
                V.bn_aggr(mv[:], bst[:]).then_inc(b_mv, 1)

            def deviation(g):
                need(dve, b_st1, g.n + 1)
                need(dve, b_nb, g.n)
                V.tensor_scalar(negm, bank[6][:, 256:257], -1.0, None, ALU.mult)
                V.tensor_tensor(dev, mv[:, 0:1], bank[6][:, 256:257], ALU.subtract).then_inc(b_dev, 1)
                need(dve, b_dev, g.n + 1)
                V.scalar_tensor_tensor(wv, dev, dev, mv[:, 1:2], ALU.mult, ALU.add).then_inc(b_w, 1)

            def plus_eps(g):
                need(dve, b_st2, g.n + 1)
                V.tensor_scalar(ve, bank[6][:, 257:258], EPS, None, ALU.add).then_inc(b_ve, 1)

            def best(g, k):
                n = NT * g.n + k
                need(dve, b_rl, n + 1)
                need(dve, b_mi, n - 3)
                hold(dve, "dve", g.n)
                V.tensor_tensor_reduce(out=Fm[:, k % 4], in0=bank[2 * (k % 2)][:], in1=R[:, k % 2], scale=1.0,
                                       scalar=-3.0e38, op0=ALU.add, op1=ALU.max,
                                       accum_out=mx[:, k % 4:k % 4 + 1]).then_inc(b_ttr, 1)

            def find(g, k):
                n = NT * g.n + k
                need(dve, b_ttr, n + 1)
                if k == 0:
                    two = Group(g.i, g.r - 2)
                    need(dve, gath[two.buf4], 16 * NT * (two.quarter + 1))
                hold(dve, "dve", g.n)
                V.max_index(idx[:, g.buf2, k], mx[:, k % 4:k % 4 + 1].broadcast_to([P, 8]),
                            Fm[:, k % 4]).then_inc(b_mi, 1)

            def settle(g):
                need(dve, b_p, g.n + 1)
                V.tensor_reduce(dot[:], prod[:], AX_X, ALU.add).then_inc(b_red, 1)
                need(dve, b_red, g.n + 1)
                V.tensor_tensor(odd[:], dot[:], q[:, g.buf2, :, 3 * D], ALU.is_gt).then_inc(b_sel, 1)
                need(dve, b_sel, g.n + 1)
                hold(dve, "dve", g.n)
                V.copy_predicated(q[:, g.buf2, :, 0:D], odd[:].unsqueeze(2).broadcast_to([P, NT, D]),
                                  q[:, g.buf2, :, D:2 * D]).then_inc(b_pr, 1)

            def body_b(i):
                for r in range(U):
                    g, before, after = Group(i, r), Group(i, r - 1), Group(i, r + 1)
                    for k in range(NT):
                        best(g, k)
                        if k > 0:
                            find(g, k - 1)
                        elif before.exists():
                            find(before, NT - 1)
                        if after.exists():
                            if k == 3:
                                residual(after)
                            if k == 5:
                                deviation(after)
                            if k == 7:
                                plus_eps(after)
                        if k == 9 and before.exists():
                            settle(before)

            residual(Group(0, 0))
            deviation(Group(0, 0))
            plus_eps(Group(0, 0))
            body_b(0)
            with dve.Fori(1, NI - 1) as i:
                body_b(i)
            body_b(NI - 1)
            find(Group(NI - 1, U - 1), NT - 1)
            settle(Group(NI - 1, U - 1))

        @block.gpsimd
        def _(pool):
            G = nc.gpsimd
            pool.wait_ge(amax_in, 1)
            G.partition_all_reduce(amax, amax0, P, RMAX).then_inc(amax_all, 1)
            pool.wait_ge(s_ve, 1)
            G.tensor_tensor(rstd_all[:], var_all[:], mhalf[:], ALU.pow).then_inc(s_rstd, 1)

            def norm_scale(g):
                need(pool, b_ve, g.n + 1)
                need(pool, b_y, g.n)
                G.tensor_tensor(rs, ve, mhalf[:, 0:1], ALU.pow).then_inc(b_rs, 1)
                need(pool, b_rs, g.n + 1)
                G.tensor_tensor(rr, rs, ymul, ALU.mult).then_inc(b_rr, 1)
                need(pool, b_rr, g.n + 1)
                G.tensor_tensor(nb, negm, rr, ALU.mult).then_inc(b_nb, 1)

            def low_half(g):
                need(pool, b_y, g.n + 1)
                G.tensor_tensor(YS[:, :, D:2 * D], Y[:, g.buf2], YS[:, :, 0:D], ALU.subtract).then_inc(b_yl, 1)

            def gather(g, k):
                need(pool, b_mi, NT * g.n + k + 1)
                if k == 0:
                    need(pool, b_fin, g.n - 1)
                hold(pool, "pool", g.n)
                G.indirect_dma_start(out=q[:, g.buf2, k], out_offset=None, in_=table,
                                     in_offset=bass.IndirectOffsetOnAxis(ap=idx[:, g.buf2, k, 0:1], axis=0)
                                     ).then_inc(gath[g.buf4], 16)

            def products(g):
                need(pool, gath[g.buf4], 16 * NT * (g.quarter + 1))
                need(pool, b_red, g.n)
                G.tensor_tensor(prod[:], q[:, g.buf2, :, 2 * D:3 * D], Y[:, g.buf2], ALU.mult).then_inc(b_p, 1)

            def finish(g):
                need(pool, b_pr, g.n + 1)
                xg = X[:, g.buf4].rearrange("p (k d) -> p k d", d=D)
                G.tensor_tensor(xg, xg, q[:, g.buf2, :, 0:D], ALU.add).then_inc(b_fin, 1)

            def body_b(i):
                for r in range(U):
                    g, before, after = Group(i, r), Group(i, r - 1), Group(i, r + 1)
                    for k in range(NT):
                        gather(g, k)
                        if before.exists():
                            if k == 2:
                                products(before)
                            if k == 12:
                                finish(before)
                        if after.exists():
                            if k == 6:
                                norm_scale(after)
                            if k == 9:
                                low_half(after)

            pool.wait_ge(tab_out, 16)
            norm_scale(Group(0, 0))
            low_half(Group(0, 0))
            body_b(0)
            with pool.Fori(1, NI - 1) as i:
                body_b(i)
            body_b(NI - 1)
            products(Group(NI - 1, U - 1))
            finish(Group(NI - 1, U - 1))


def shape_constants():
    def cosines(freq, pos, n, weight_of):
        ends = (weight_of == 0) | (weight_of == n - 1)
        return np.cos(np.pi * np.multiply.outer(pos, freq) / (n - 1)) * np.where(ends, 1.0, 2.0)

    kx = np.concatenate([np.arange(MX // 2), np.arange(H - MX // 2, H)])
    ky = np.arange(MY)
    h, w = np.arange(H), np.arange(W)
    fh = cosines(kx, h, H, h[:, None]).reshape(P, T2, MX)
    fw = cosines(ky, w, W, w[:, None]).reshape(2, P, MY).transpose(1, 0, 2)
    ih = cosines(kx, h, H, kx[None, :]).reshape(P, T2, MX).transpose(2, 1, 0).reshape(MX, T2 * P)
    iw = np.tile(cosines(ky, w, W, ky[None, :]).T, (CG, 1))
    gm = (np.arange(P)[:, None] % C) // CG == np.arange(C // CG)[None, :]
    rm = np.arange(P)[:, None] == D + np.arange(3)[None, :]
    return [np.ascontiguousarray(a, dtype=np.float32) for a in (fh, fw, ih, iw, np.eye(P), gm, rm)]


def kernel(x, L0_conv_weights1, L0_conv_weights2, L1_conv_embeddings):
    import concourse.bacc as bacc
    from concourse.bass_utils import run_bass_kernel_spmd

    nc = bacc.Bacc("TRN2", target_bir_lowering=False, num_devices=1)
    given = [x, L0_conv_weights1, L0_conv_weights2, L1_conv_embeddings] + shape_constants()
    names = ["x", "w1", "w2", "emb", "c_fh", "c_fw", "c_ih", "c_iw", "c_id", "c_gm", "c_rm"]
    arrays = {n: np.ascontiguousarray(a) for n, a in zip(names, given)}
    args = [nc.dram_tensor(n, a.shape, F32, kind="ExternalInput").ap() for n, a in arrays.items()]
    args.append(nc.dram_tensor("y", (B, C, H, W), F32, kind="ExternalOutput").ap())
    program(nc, *args)
    return run_bass_kernel_spmd(nc, [arrays], core_ids=[0]).results[0]["y"]
```

```python
from contextlib import ExitStack

import numpy as np

import concourse.bass as bass
from concourse import mybir

ALU = mybir.AluOpType
ACT = mybir.ActivationFunctionType
AX_X = mybir.AxisListType.X
F32 = mybir.dt.float32
F16 = mybir.dt.float16
I32 = mybir.dt.int32
U32 = mybir.dt.uint32
RMAX = bass.bass_isa.ReduceOp.max

P = 128
B, C, H, W = 8, 64, 256, 256
CG = 2
NG = B * C // CG
U = 4
NI = NG // U
T2 = H // P
MX, MY = 64, 32
HALF = MX // 2 * MY
CH = 64
NCH = HALF // CH
D = 64
K = 1024
NP = K // 2
NT = CG * H * W // D // P
ROW = 3 * D + 4
DC = float((2 * (H - 1)) * (2 * (W - 1)))
EPS = 1e-5
E_SCALE = 2.0 ** 14
Y_SCALE = 2.0 ** 7
ONE = 2.0 ** 15


class Group:

    def __init__(self, i, r):
        self.i, self.r = i + r // U if isinstance(i, int) else i, r % U if isinstance(i, int) else r
        self.n = U * self.i + self.r
        self.buf4 = r % 4
        self.buf2 = r % 2
        self.quarter = self.i + self.r // 4 if not isinstance(i, int) else self.n // 4
        self.half = 2 * self.i + self.r // 2 if not isinstance(i, int) else self.n // 2

    def exists(self):
        return not isinstance(self.n, int) or 0 <= self.n < NG


def need(eng, sem, count):
    if not isinstance(count, int) or count > 0:
        eng.wait_ge(sem, count)


def program(nc, x, w1, w2, emb, c_fh, c_fw, c_ih, c_iw, c_id, c_gm, c_rm, out):
    spec = nc.dram_tensor("spec", [B, C, MX * MY], F32, kind="Internal").ap()
    mixed = nc.dram_tensor("mixed", [B, C, MX * MY], F32, kind="Internal").ap()
    table = nc.dram_tensor("table", [NP, ROW], F32, kind="Internal").ap()

    x_g = x.rearrange("b (g i) (p t) w -> (b g) p i (t w)", i=CG, t=T2)
    out_g = out.rearrange("b (g i) (p t) w -> (b g) p i (t w)", i=CG, t=T2)
    spec_g = spec.rearrange("b (g i) (x y) -> (b g) (i x) y", i=CG, y=MY)
    spec_c = spec.rearrange("b c m -> c b m")
    mixed_c = mixed.rearrange("b o m -> o b m")
    mixed_g = mixed.rearrange("b (g i) (x y) -> (b g) x i y", i=CG, y=MY)
    w_m = [w.rearrange("i o x y -> i o (x y)") for w in (w1, w2)]

    with ExitStack() as ctx:
        def sb(name, shape, dt=F32):
            return ctx.enter_context(nc.sbuf_tensor(name, shape, dt))

        def sem(name):
            return ctx.enter_context(nc.semaphore(name))

        bank = [ctx.enter_context(nc.psum_tensor(f"bank{n}", [P, 512], F32)) for n in range(8)]

        fh = sb("fh", [P, T2, MX])
        fw = sb("fw", [P, 2, MY])
        ih = sb("ih", [MX, T2 * P])
        iw = sb("iw", [CG * MY, W])
        ident = sb("ident", [P, P])
        gmask = sb("gmask", [P, C // CG])
        rmask = sb("rmask", [P, 3])
        ident16 = sb("ident16", [P, P], F16)
        avg = sb("avg", [P, P])
        ones = sb("ones", [D, P])
        mhalf = sb("mhalf", [P, NG])
        avg_all = sb("avg_all", [P, P])
        consts = ((fh, c_fh), (fw, c_fw), (ih, c_ih), (iw, c_iw), (ident, c_id), (gmask, c_gm), (rmask, c_rm))

        E = sb("E", [P, NP, 2])
        S = sb("S", [P, 2, NP])
        S2 = sb("S2", [P, 2, NP])
        eh = sb("eh", [P, 2, NP], F16)
        el = sb("el", [P, 2, NP], F16)
        part = sb("part", [P, 2, NP], F16)
        tb = sb("tb", [P, 4, ROW])
        tsq = sb("tsq", [P, 4, 2, D])
        tnorm = sb("tnorm", [P, 4, 2])
        sc = sb("sc", [P, 8])
        amax0, amax, inv_a, inv_s, ymul, ymulh, bscale, escale = (sc[:, n:n + 1] for n in range(8))

        X = sb("X", [P, 4, CG * T2 * W])
        st = sb("st", [P, U, 2, 6])
        mvs = sb("mvs", [P, U, 2])
        mv_all = sb("mv_all", [P, NG, 2])
        dev_all = sb("dev_all", [P, NG])
        var_all = sb("var_all", [P, NG])
        rstd_all = sb("rstd_all", [P, NG])
        mean_all = sb("mean_all", [P, NG])
        sel8 = sb("sel8", [P, B, C // CG])
        r_c = sb("r_c", [P, B])
        m_c = sb("m_c", [P, B])
        dc_fix = sb("dc_fix", [P, NCH * B])
        Us = sb("Us", [MX, 2, 512])
        UTs = sb("UTs", [P, 2, 256])
        Fs = sb("Fs", [P, U, MY])
        Wc = sb("Wc", [P, 2, C, CH])
        Xc = sb("Xc", [P, 2, B, CH])
        Oc = sb("Oc", [P, 2, B, CH])
        M = sb("M", [MX, 2, CG * MY])
        Ts = sb("Ts", [CG * MY, T2 * P])
        sums = sb("sums", [P, 3])
        squares = sb("squares", [P, CG * T2 * W], F16)
        small = sb("small", [P, 8])
        mean1, delta, delta2, ve, rs, rr, nb = (small[:, n:n + 1] for n in range(7))
        YS = sb("YS", [P, NT, 2 * D], F16)
        Y = sb("Y", [P, 4, NT, D])
        t1 = sb("t1", [P, 2, NT, P], F16)
        t2 = sb("t2", [P, 2, NT, P], F16)
        R = sb("R", [P, 4, NP])
        Fm = sb("Fm", [P, 4, NP])
        mx = sb("mx", [P, 4])
        idx = sb("idx", [P, 2, NT, 8], U32)
        q = sb("q", [P, 2, NT, ROW])
        prod = sb("prod", [P, NT, D])
        dot = sb("dot", [P, NT])
        odd = sb("odd", [P, NT], I32)

        consts_in = sem("consts_in")
        emb_in = sem("emb_in")
        held = {n: sem(f"held_{n}") for n in ("pe", "act", "dve", "pool")}
        dve_step = sem("dve_step")
        ids_ready = sem("ids_ready")
        amax_in = sem("amax_in")
        amax_all = sem("amax_all")
        esq_in = sem("esq_in")
        esq_done = sem("esq_done")
        tab_tr = sem("tab_tr")
        tab_ready = sem("tab_ready")
        tab_out = sem("tab_out")
        codes_ready = sem("codes_ready")

        xa_in = [sem(f"xa_in{n}") for n in range(U)]
        a_h, a_u, a_tr, a_ut, a_w, a_f = (sem(n) for n in ("a_h", "a_u", "a_tr", "a_ut", "a_w", "a_f"))
        a_bn, a_mv, a_mvc = (sem(n) for n in ("a_bn", "a_mv", "a_mvc"))
        fs_out = [sem(f"fs_out{n}") for n in range(U)]
        s_mean, s_dev, s_var, s_ve, s_rstd = (sem(n) for n in ("s_mean", "s_dev", "s_var", "s_ve", "s_rstd"))
        w_in = [sem(f"w_in{n}") for n in range(2)]
        xs_in = [sem(f"xs_in{n}") for n in range(2)]
        m_sc, m_x, m_mm, m_ev = (sem(n) for n in ("m_sc", "m_x", "m_mm", "m_ev"))
        o_out = [sem(f"o_out{n}") for n in range(2)]

        x_in = [sem(f"x_in{n}") for n in range(4)]
        m_in = [sem(f"m_in{n}") for n in range(2)]
        y_out = [sem(f"y_out{n}") for n in range(4)]
        gath = [sem(f"gath{n}") for n in range(4)]
        b_inv, b_t, b_conv, b_x1, b_sq, b_st, b_mean, b_delta, b_delta2, b_ve, b_rs, b_rr, b_nb = (
            sem("b_" + n) for n in "inv t conv x1 sq st mean delta delta2 ve rs rr nb".split())
        b_y, b_yl, b_tp, b_te, b_sc, b_rl, b_ttr, b_mi, b_p, b_red, b_sel, b_pr, b_fin = (
            sem("b_" + n) for n in "y yl tp te sc rl ttr mi p red sel pr fin".split())

        def hold(eng, name, count):
            if not isinstance(count, int):
                eng.sem_inc(held[name], 1)

        block = ctx.enter_context(nc.Block())

        @block.sync
        def _(sp):
            sp.dma_start(E[0:D], emb.rearrange("d (j e) -> d j e", e=2)).then_inc(emb_in, 16)
            sp.dma_start(E[D:P], emb.rearrange("d (j e) -> d j e", e=2)).then_inc(emb_in, 16)
            for tile, src in consts:
                sp.dma_start(tile[:], src).then_inc(consts_in, 16)

            def load_weights(c, v):
                for n in range(2):
                    sp.dma_start(Wc[64 * n:64 * n + 64, v], w_m[n][:, :, bass.ds(c * CH, CH)]).then_inc(w_in[v], 16)

            def group_a(g):
                need(sp, a_h, g.n - 3)
                need(sp, a_bn, g.n - 3)
                sp.dma_start(X[:, g.buf4].rearrange("p (i f) -> p i f", i=CG), x_g[g.n]).then_inc(xa_in[g.buf4], 16)

            def store_a(g):
                need(sp, a_f, g.n + 1)
                sp.dma_start(spec_g[g.n], Fs[:, g.buf4]).then_inc(fs_out[g.buf4], 16)

            for r in range(U):
                group_a(Group(0, r))
            load_weights(0, 0)
            load_weights(1, 1)
            with sp.Fori(1, NI) as i:
                for r in range(U):
                    store_a(Group(i, r - U))
                    group_a(Group(i, r))
            for r in range(U):
                store_a(Group(NI - 1, r))
            sp.wait_ge(tab_ready, 1)
            sp.dma_start(table.rearrange("(c p) w -> p c w", p=P), tb[:]).then_inc(tab_out, 16)
            for n in range(U):
                sp.wait_ge(fs_out[n], 16 * NI)

            def load_m(i, v):
                c = 2 * i + v
                need(sp, m_mm, c - 1)
                for n in range(2):
                    sp.dma_start(Xc[64 * n:64 * n + 64, v],
                                 spec_c[:, :, bass.ds(c * CH + n * HALF, CH)]).then_inc(xs_in[v], 16)
                if not (isinstance(i, int) and i == 0):
                    load_weights(c, v)

            load_m(0, 0)
            load_m(0, 1)
            with sp.Fori(1, NCH // 2) as i:
                for v in range(2):
                    load_m(i, v)

            def load_x(g):
                need(sp, y_out[g.buf4], 16 * g.quarter)
                sp.dma_start(X[:, g.buf4].rearrange("p (i f) -> p i f", i=CG), x_g[g.n]).then_inc(x_in[g.buf4], 16)

            def load_modes(g):
                need(sp, b_inv, g.n - 1)
                sp.dma_start(M[:, g.buf2].rearrange("p (i y) -> p i y", i=CG), mixed_g[g.n]).then_inc(m_in[g.buf2], 16)

            def store_y(g):
                need(sp, b_fin, g.n + 1)
                sp.dma_start(out_g[g.n], X[:, g.buf4].rearrange("p (i f) -> p i f", i=CG)).then_inc(y_out[g.buf4], 16)

            sp.wait_ge(a_h, NG)
            sp.wait_ge(a_bn, NG)
            for r in range(3):
                load_x(Group(0, r))
            for n in range(2):
                sp.wait_ge(o_out[n], 32 * (NCH // 2))
            for r in range(3):
                load_modes(Group(0, r))

            def body(i):
                for r in range(U):
                    if Group(i, r + 3).exists():
                        load_modes(Group(i, r + 3))
                    if Group(i, r - 1).exists():
                        store_y(Group(i, r - 1))
                    if Group(i, r + 3).exists():
                        load_x(Group(i, r + 3))

            body(0)
            with sp.Fori(1, NI - 1) as i:
                body(i)
            body(NI - 1)
            store_y(Group(NI - 1, U - 1))
            for n in range(4):
                sp.wait_ge(y_out[n], 16 * NI)

        @block.tensor
        def _(pe):
            pe.wait_ge(consts_in, 16 * len(consts))
            pe.wait_ge(ids_ready, 1)

            pe.wait_ge(esq_in, 1)
            for e in range(2):
                last = nc.tensor.matmul(bank[e][:], ones[:], S2[0:D, e], start=True, stop=True)
            last.then_inc(esq_done, 1)
            for c in range(4):
                for e in range(2):
                    last = nc.tensor.transpose(bank[2][:, (2 * c + e) * D:(2 * c + e + 1) * D],
                                               E[0:D, c * P:(c + 1) * P, e], ident[0:D, 0:D])
            last.then_inc(tab_tr, 1)
            pe.wait_ge(codes_ready, 1)

            def dct_h(g):
                need(pe, xa_in[g.buf4], 16 * (g.quarter + 1))
                need(pe, a_u, g.n - 1)
                xg = X[:, g.buf4].rearrange("p (i t w) -> p t i w", i=CG, t=T2)
                for t in range(T2):
                    last = nc.tensor.matmul(bank[g.buf2][0:MX], fh[:, t], xg[:, t], start=t == 0, stop=t == T2 - 1)
                last.then_inc(a_h, 1)

            def turn(g):
                need(pe, a_u, g.n + 1)
                need(pe, a_ut, g.n - 1)
                hold(pe, "pe", g.n)
                for wc in range(2):
                    for i in range(CG):
                        last = nc.tensor.transpose(bank[2 + g.buf2][:, (2 * wc + i) * MX:(2 * wc + i + 1) * MX],
                                                   Us[:, g.buf2, i * W + wc * P:i * W + (wc + 1) * P],
                                                   ident[0:MX, 0:MX])
                last.then_inc(a_tr, 1)

            def dct_w(g):
                need(pe, a_ut, g.n + 1)
                need(pe, a_f, g.n - 1)
                for wc in range(2):
                    last = nc.tensor.matmul(bank[4 + g.buf2][:, 0:MY], UTs[:, g.buf2, wc * P:(wc + 1) * P],
                                            fw[:, wc], start=wc == 0, stop=wc == 1)
                last.then_inc(a_w, 1)

            def body_a(i):
                for r in range(U):
                    dct_h(Group(i, r))
                    if Group(i, r - 2).exists():
                        dct_w(Group(i, r - 2))
                    if Group(i, r - 1).exists():
                        turn(Group(i, r - 1))

            body_a(0)
            with pe.Fori(1, NI) as i:
                body_a(i)
            dct_w(Group(NI - 1, U - 2))
            turn(Group(NI - 1, U - 1))
            dct_w(Group(NI - 1, U - 1))

            pe.wait_ge(a_mvc, NI)
            nc.tensor.matmul(bank[6][:, 0:NG], avg[:], mv_all[:, :, 0], start=True, stop=True).then_inc(s_mean, 1)
            pe.wait_ge(s_dev, 1)
            nc.tensor.matmul(bank[7][:, 0:NG], avg[:], dev_all[:], start=True, stop=True).then_inc(s_var, 1)

            pe.wait_ge(a_ut, NG)
            pe.wait_ge(a_f, NG)

            def mix(i, v):
                c = 2 * i + v
                need(pe, w_in[v], 32 * (i + 1))
                need(pe, m_x, c + 1)
                need(pe, m_ev, c - 1)
                hold(pe, "pe", i)
                for m in range(CH):
                    for n in range(2):
                        half = slice(64 * n, 64 * n + 64)
                        last = nc.tensor.matmul(bank[2 * v + n][half, m * B:(m + 1) * B], Wc[half, v, :, m],
                                                Xc[half, v, :, m], start=True, stop=True)
                last.then_inc(m_mm, 1)

            mix(0, 0)
            mix(0, 1)
            with pe.Fori(1, NCH // 2) as i:
                for v in range(2):
                    mix(i, v)

            pe.wait_ge(m_ev, NCH)
            pe.wait_ge(s_ve, 1)
            tp = bank[7][:].bitcast(F16).rearrange("p (k f) -> p k f", k=NT // 2)

            def inverse_h(g):
                need(pe, m_in[g.buf2], 16 * (g.half + 1))
                need(pe, b_ve, g.n)
                hold(pe, "pe", g.n)
                nc.tensor.matmul(bank[6][0:CG * MY, 0:T2 * P], M[:, g.buf2], ih[:], start=True,
                                 stop=True).then_inc(b_inv, 1)

            def inverse_w(g, i):
                need(pe, x_in[g.buf4], 16 * (g.quarter + 1))
                need(pe, b_t, g.n + 1)
                need(pe, b_x1, 2 * g.n + i)
                nc.tensor.matmul(bank[6][:], ident[:], X[:, g.buf4, 512 * i:512 * (i + 1)], start=True, stop=False)
                rows = slice(i * MY, (i + 1) * MY)
                for t in range(T2):
                    last = nc.tensor.matmul(bank[6][:, t * W:(t + 1) * W], Ts[rows, t * P:(t + 1) * P],
                                            iw[rows], start=False, stop=t == T2 - 1)
                last.then_inc(b_conv, 1)

            def statistics(g):
                need(pe, b_sq, g.n + 1)
                nc.tensor.matmul(bank[6][:, 0:3], avg_all[:], sums[:], start=True, stop=True).then_inc(b_st, 1)

            def turn_y(g, half):
                need(pe, b_yl, g.n + 1)
                need(pe, b_te, 2 * g.n + half)
                for k in range(NT // 2):
                    last = nc.tensor.transpose(tp[:, k], YS[:, half * (NT // 2) + k], ident16[:])
                last.then_inc(b_tp, 1)

            def scores(g, k):
                n = NT * g.n + k
                if k % (NT // 2) == 0:
                    need(pe, b_te, 2 * g.n + 1 + k // (NT // 2))
                need(pe, b_ttr, n - 3)
                need(pe, b_rl, n - 1)
                for rows, tile, codes in ((P, t1, eh), (D + 3, t2, el)):
                    for e in range(2):
                        last = nc.tensor.matmul(bank[4 + k % 2 if e else k % 4][:], tile[0:rows, g.buf2, k],
                                                codes[0:rows, e], start=rows == P, stop=rows != P)
                last.then_inc(b_sc, 1)

            def body_b(i):
                for r in range(U):
                    g, one, two = Group(i, r), Group(i, r + 1), Group(i, r + 2)
                    for k in range(NT):
                        scores(g, k)
                        if two.exists():
                            if k == 1:
                                inverse_h(two)
                            if k == 4:
                                inverse_w(two, 0)
                            if k == 7:
                                inverse_w(two, 1)
                            if k == 11:
                                statistics(two)
                        if one.exists():
                            if k == 10:
                                turn_y(one, 0)
                            if k == 13:
                                turn_y(one, 1)

            for r in range(2):
                inverse_h(Group(0, r))
                inverse_w(Group(0, r), 0)
                inverse_w(Group(0, r), 1)
                statistics(Group(0, r))
            turn_y(Group(0, 0), 0)
            turn_y(Group(0, 0), 1)
            body_b(0)
            with pe.Fori(1, NI - 1) as i:
                body_b(i)
            body_b(NI - 1)

        @block.scalar
        def _(act):
            def take_u(g):
                need(act, a_h, g.n + 1)
                need(act, a_tr, g.n - 1)
                nc.scalar.copy(Us[:, g.buf2], bank[g.buf2][0:MX]).then_inc(a_u, 1)

            def take_f(g):
                need(act, a_w, g.n + 1)
                need(act, fs_out[g.buf4], 16 * g.quarter)
                nc.scalar.copy(Fs[:, g.buf4], bank[4 + g.buf2][:, 0:MY]).then_inc(a_f, 1)

            def body_a(i):
                for r in range(U):
                    take_u(Group(i, r))
                    if Group(i, r - 2).exists():
                        take_f(Group(i, r - 2))

            body_a(0)
            with act.Fori(1, NI) as i:
                body_a(i)
            take_f(Group(NI - 1, U - 2))
            take_f(Group(NI - 1, U - 1))

            def take_mix(i, v):
                c = 2 * i + v
                need(act, m_mm, c + 1)
                need(act, o_out[v], 32 * i)
                for n in range(2):
                    half = slice(64 * n, 64 * n + 64)
                    last = nc.scalar.copy(Oc[half, v].rearrange("p b m -> p m b"),
                                          bank[2 * v + n][half].rearrange("p (m b) -> p m b", b=B))
                last.then_inc(m_ev, 1)
                act.wait_ge(m_ev, c + 1)
                for n in range(2):
                    act.dma_start(mixed_c[:, :, bass.ds(c * CH + n * HALF, CH)],
                                  Oc[64 * n:64 * n + 64, v]).then_inc(o_out[v], 16)

            take_mix(0, 0)
            take_mix(0, 1)
            with act.Fori(1, NCH // 2) as i:
                for v in range(2):
                    take_mix(i, v)

            tp = bank[7][:].bitcast(F16).rearrange("p (k f) -> p k f", k=NT // 2)

            def take_t(g):
                need(act, b_inv, g.n + 1)
                need(act, b_conv, 2 * g.n)
                nc.scalar.copy(Ts[:], bank[6][0:CG * MY, 0:T2 * P]).then_inc(b_t, 1)

            def take_x(g, i):
                need(act, b_conv, 2 * g.n + i + 1)
                need(act, b_st, g.n)
                nc.scalar.activation(X[:, g.buf4, 512 * i:512 * (i + 1)], bank[6][:], ACT.Identity,
                                     accum_out=sums[:, i:i + 1]).then_inc(b_x1, 1)

            def square_sum(g):
                need(act, b_x1, 2 * g.n + 2)
                nc.scalar.activation(squares[:], X[:, g.buf4], ACT.Square, scale=-1.0,
                                     bias=mean_all[:, bass.ds(g.n, 1)], accum_out=sums[:, 2:3]).then_inc(b_sq, 1)

            def normalise(g):
                need(act, b_nb, g.n + 1)
                need(act, b_tp, 2 * g.n)
                need(act, b_p, g.n - 3)
                xg = X[:, g.buf4].rearrange("p (k d) -> p k d", d=D)
                nc.scalar.activation(YS[:, :, 0:D], xg, ACT.Identity, bias=nb, scale=rr)
                nc.scalar.activation(Y[:, g.buf4], xg, ACT.Identity, bias=nb, scale=rr).then_inc(b_y, 1)

            def take_y(g, half):
                need(act, b_tp, 2 * g.n + half + 1)
                need(act, b_sc, NT * (g.n - 1))
                ks = slice(half * (NT // 2), (half + 1) * (NT // 2))
                nc.scalar.copy(t1[:, g.buf2, ks], tp)
                nc.scalar.copy(t2[0:D, g.buf2, ks], tp[0:D]).then_inc(b_te, 1)

            def relu(g, k):
                n = NT * g.n + k
                need(act, b_sc, n + 1)
                need(act, b_ttr, n - 3)
                nc.scalar.activation(R[:, k % 4], bank[4 + k % 2][:], ACT.Relu).then_inc(b_rl, 1)

            def body_b(i):
                for r in range(U):
                    g, one, two = Group(i, r), Group(i, r + 1), Group(i, r + 2)
                    for k in range(NT):
                        relu(g, k)
                        if one.exists():
                            if k == 1:
                                normalise(one)
                            if k == 11:
                                take_y(one, 0)
                            if k == 14:
                                take_y(one, 1)
                        if two.exists():
                            if k == 2:
                                take_t(two)
                            if k == 5:
                                take_x(two, 0)
                            if k == 8:
                                take_x(two, 1)
                            if k == 9:
                                square_sum(two)

            act.wait_ge(codes_ready, 1)
            for r in range(2):
                take_t(Group(0, r))
                take_x(Group(0, r), 0)
                take_x(Group(0, r), 1)
                square_sum(Group(0, r))
                if r == 0:
                    normalise(Group(0, 0))
            take_y(Group(0, 0), 0)
            take_y(Group(0, 0), 1)
            body_b(0)
            with act.Fori(1, NI - 1) as i:
                body_b(i)
            body_b(NI - 1)

        @block.vector
        def _(dve):
            steps = [0]

            def then(ins):
                steps[0] += 1
                ins.then_inc(dve_step, 1)
                dve.wait_ge(dve_step, steps[0])

            V = nc.vector
            V.memset(avg[:], 1.0 / P)
            V.memset(avg_all[:], 1.0 / (P * CG * T2 * W))
            V.memset(ones[:], 1.0)
            V.memset(mhalf[:], -0.5)
            V.memset(t2[D:P], ONE)
            V.memset(dc_fix[:], 0.0)
            V.memset(tb[:], 0.0)
            dve.wait_ge(consts_in, 16 * len(consts))
            V.tensor_copy(ident16[:], ident[:]).then_inc(ids_ready, 1)

            dve.wait_ge(emb_in, 32)
            Ef = E[:].rearrange("p j e -> p (j e)")
            V.tensor_reduce(amax0, Ef, AX_X, ALU.max, apply_absolute_value=True).then_inc(amax_in, 1)
            V.tensor_tensor(S2[:].rearrange("p e j -> p j e"), E[:], E[:], ALU.mult).then_inc(esq_in, 1)
            dve.wait_ge(amax_all, 1)
            then(V.tensor_scalar(amax, amax, 1e-30, None, ALU.max))
            then(V.reciprocal(inv_a, amax))
            then(V.tensor_scalar(inv_s, amax, 1.0 / 16.0, 1.0, ALU.mult, ALU.max))
            then(V.reciprocal(inv_s, inv_s))
            V.tensor_scalar(ymul, inv_s, Y_SCALE, None, ALU.mult)
            V.tensor_scalar(ymulh, inv_s, Y_SCALE / 2, None, ALU.mult)
            V.tensor_scalar(escale, inv_a, E_SCALE, None, ALU.mult)
            then(V.scalar_tensor_tensor(bscale, inv_a, -Y_SCALE * E_SCALE / 2 / ONE, inv_s, ALU.mult, ALU.mult))
            then(V.tensor_tensor(S[:, 1], E[:, :, 1], E[:, :, 0], ALU.subtract))
            V.tensor_scalar(S[:, 0], E[:, :, 0], escale, None, ALU.mult)
            then(V.tensor_scalar(S[:, 1], S[:, 1], escale, None, ALU.mult))
            then(V.tensor_copy(eh[:], S[:]))
            then(V.tensor_tensor(el[0:D], S[0:D], eh[0:D], ALU.subtract))
            dve.wait_ge(esq_done, 1)
            then(V.tensor_copy(S[:, 0], bank[0][:]))
            then(V.tensor_tensor(S[:, 1], bank[1][:], S[:, 0], ALU.subtract))
            then(V.tensor_scalar(S[:], S[:], bscale, None, ALU.mult))
            for n in range(3):
                then(V.tensor_copy(part[:], S[:]))
                if n == 0:
                    then(V.tensor_scalar(el[D:P], part[D:P], rmask[D:P, 0:1], None, ALU.mult))
                else:
                    then(V.scalar_tensor_tensor(el[D:P], part[D:P], rmask[D:P, n:n + 1], el[D:P], ALU.mult, ALU.add))
                if n < 2:
                    then(V.tensor_tensor(S[:], S[:], part[:], ALU.subtract))
            dve.wait_ge(tab_tr, 1)
            tt = bank[2][:].rearrange("p (c e d) -> p c e d", c=4, e=2)
            V.tensor_copy(tb[:, :, 0:D], tt[:, :, 0])
            then(V.tensor_copy(tb[:, :, D:2 * D], tt[:, :, 1]))
            V.tensor_tensor(tb[:, :, 2 * D:3 * D], tb[:, :, D:2 * D], tb[:, :, 0:D], ALU.subtract)
            te = tb[:, :, 0:2 * D].rearrange("p c (e d) -> p c e d", e=2)
            then(V.tensor_tensor(tsq[:], te, te, ALU.mult))
            then(V.tensor_reduce(tnorm[:], tsq[:], AX_X, ALU.add))
            then(V.tensor_tensor(tnorm[:, :, 0], tnorm[:, :, 1], tnorm[:, :, 0], ALU.subtract))
            then(V.tensor_scalar(tb[:, :, 3 * D], tnorm[:, :, 0], ymulh, None, ALU.mult))
            dve.sem_inc(tab_ready, 1)
            dve.sem_inc(codes_ready, 2)

            def stats(g):
                need(dve, xa_in[g.buf4], 16 * (g.quarter + 1))
                for n in range(2):
                    last = V.bn_stats(st[:, g.buf4, n], X[:, g.buf4, 512 * n:512 * (n + 1)])
                last.then_inc(a_bn, 1)

            def join(g):
                need(dve, a_bn, g.n + 1)
                need(dve, a_mvc, g.quarter)
                hold(dve, "dve", g.n)
                V.bn_aggr(mvs[:, g.buf4], st[:, g.buf4]).then_inc(a_mv, 1)

            def take_ut(g):
                need(dve, a_tr, g.n + 1)
                need(dve, a_w, g.n - 1)
                V.tensor_copy(UTs[:, g.buf2], bank[2 + g.buf2][:, 0:256]).then_inc(a_ut, 1)

            def body_a(i):
                for r in range(U):
                    stats(Group(i, r))
                    if Group(i, r - 1).exists():
                        take_ut(Group(i, r - 1))
                    join(Group(i, r))
                need(dve, a_mv, U * (i + 1))
                V.tensor_copy(mv_all[:, bass.ds(U * i, U), :], mvs[:]).then_inc(a_mvc, 1)

            body_a(0)
            with dve.Fori(1, NI) as i:
                body_a(i)
            take_ut(Group(NI - 1, U - 1))

            dve.wait_ge(s_mean, 1)
            then(V.tensor_copy(mean_all[:], bank[6][:, 0:NG]))
            then(V.tensor_tensor(dev_all[:], mv_all[:, :, 0], mean_all[:], ALU.subtract))
            then(V.tensor_tensor(dev_all[:], dev_all[:], dev_all[:], ALU.mult))
            V.tensor_tensor(dev_all[:], dev_all[:], mv_all[:, :, 1], ALU.add).then_inc(s_dev, 1)
            dve.wait_ge(s_var, 1)
            V.tensor_scalar(var_all[:], bank[7][:, 0:NG], EPS, None, ALU.add).then_inc(s_ve, 1)
            dve.wait_ge(s_rstd, 1)
            gm = gmask[:].unsqueeze(1).broadcast_to([P, B, C // CG])
            then(V.tensor_tensor(sel8[:], rstd_all[:].rearrange("p (b g) -> p b g", b=B), gm, ALU.mult))
            then(V.tensor_reduce(r_c[:], sel8[:], AX_X, ALU.add))
            then(V.tensor_tensor(sel8[:], mean_all[:].rearrange("p (b g) -> p b g", b=B), gm, ALU.mult))
            then(V.tensor_reduce(m_c[:], sel8[:], AX_X, ALU.add))
            then(V.scalar_tensor_tensor(dc_fix[0:C, 0:B], m_c[0:C], DC, r_c[0:C], ALU.mult, ALU.mult))

            def scale(i, v):
                c = 2 * i + v
                need(dve, xs_in[v], 32 * (i + 1))
                V.tensor_tensor(Xc[:, v], Xc[:, v], r_c[:].unsqueeze(2).broadcast_to([P, B, CH]),
                                ALU.mult).then_inc(m_sc, 1)
                dve.wait_ge(m_sc, c + 1)
                V.tensor_tensor(Xc[:, v, :, 0], Xc[:, v, :, 0], dc_fix[:, bass.ds(c * B, B)],
                                ALU.subtract).then_inc(m_x, 1)

            scale(0, 0)
            scale(0, 1)
            with dve.Fori(1, NCH // 2) as i:
                for v in range(2):
                    scale(i, v)

            def moments(g):
                need(dve, b_st, g.n + 1)
                need(dve, b_nb, g.n)
                V.tensor_reduce(mean1, bank[6][:, 0:2], AX_X, ALU.add).then_inc(b_mean, 1)
                need(dve, b_mean, g.n + 1)
                V.tensor_tensor(delta, mean1, mean_all[:, bass.ds(g.n, 1)], ALU.subtract).then_inc(b_delta, 1)
                need(dve, b_delta, g.n + 1)
                V.tensor_tensor(delta2, delta, delta, ALU.mult).then_inc(b_delta2, 1)
                need(dve, b_delta2, g.n + 1)
                V.scalar_tensor_tensor(ve, bank[6][:, 2:3], EPS, delta2, ALU.add, ALU.subtract).then_inc(b_ve, 1)

            def norm_scale(g):
                need(dve, b_rs, g.n + 1)
                need(dve, b_y, g.n)
                V.tensor_tensor(rr, rs, ymul, ALU.mult).then_inc(b_rr, 1)
                need(dve, b_rr, g.n + 1)
                V.scalar_tensor_tensor(nb, mean1, -1.0, rr, ALU.mult, ALU.mult).then_inc(b_nb, 1)

            def best(g, k):
                n = NT * g.n + k
                need(dve, b_rl, n + 1)
                need(dve, b_mi, n - 3)
                hold(dve, "dve", g.n)
                V.tensor_tensor_reduce(out=Fm[:, k % 4], in0=bank[k % 4][:], in1=R[:, k % 4], scale=1.0,
                                       scalar=-3.0e38, op0=ALU.add, op1=ALU.max,
                                       accum_out=mx[:, k % 4:k % 4 + 1]).then_inc(b_ttr, 1)

            def find(g, k):
                n = NT * g.n + k
                need(dve, b_ttr, n + 1)
                if k == 0:
                    two = Group(g.i, g.r - 2)
                    need(dve, gath[two.buf4], 16 * NT * (two.quarter + 1))
                hold(dve, "dve", g.n)
                V.max_index(idx[:, g.buf2, k], mx[:, k % 4:k % 4 + 1].broadcast_to([P, 8]),
                            Fm[:, k % 4]).then_inc(b_mi, 1)

            def settle(g):
                need(dve, b_p, g.n + 1)
                V.tensor_reduce(dot[:], prod[:], AX_X, ALU.add).then_inc(b_red, 1)
                need(dve, b_red, g.n + 1)
                V.tensor_tensor(odd[:], dot[:], q[:, g.buf2, :, 3 * D], ALU.is_gt).then_inc(b_sel, 1)
                need(dve, b_sel, g.n + 1)
                hold(dve, "dve", g.n)
                V.copy_predicated(q[:, g.buf2, :, 0:D], odd[:].unsqueeze(2).broadcast_to([P, NT, D]),
                                  q[:, g.buf2, :, D:2 * D]).then_inc(b_pr, 1)

            def body_b(i):
                for r in range(U):
                    g, before, two = Group(i, r), Group(i, r - 1), Group(i, r + 2)
                    for k in range(NT):
                        best(g, k)
                        if k > 0:
                            find(g, k - 1)
                        elif before.exists():
                            find(before, NT - 1)
                        if two.exists():
                            if k == 11:
                                moments(two)
                            if k == 14:
                                norm_scale(two)
                        if k == 6 and before.exists():
                            settle(before)

            for r in range(2):
                moments(Group(0, r))
                norm_scale(Group(0, r))
            body_b(0)
            with dve.Fori(1, NI - 1) as i:
                body_b(i)
            body_b(NI - 1)
            find(Group(NI - 1, U - 1), NT - 1)
            settle(Group(NI - 1, U - 1))

        @block.gpsimd
        def _(pool):
            G = nc.gpsimd
            pool.wait_ge(amax_in, 1)
            G.partition_all_reduce(amax, amax0, P, RMAX).then_inc(amax_all, 1)
            pool.wait_ge(s_ve, 1)
            G.tensor_tensor(rstd_all[:], var_all[:], mhalf[:], ALU.pow).then_inc(s_rstd, 1)

            def inverse_deviation(g):
                need(pool, b_ve, g.n + 1)
                need(pool, b_rr, g.n)
                G.tensor_tensor(rs, ve, mhalf[:, 0:1], ALU.pow).then_inc(b_rs, 1)

            def low_half(g):
                need(pool, b_y, g.n + 1)
                G.tensor_tensor(YS[:, :, D:2 * D], Y[:, g.buf4], YS[:, :, 0:D], ALU.subtract).then_inc(b_yl, 1)

            def gather(g, k):
                need(pool, b_mi, NT * g.n + k + 1)
                if k == 0:
                    need(pool, b_fin, g.n - 1)
                hold(pool, "pool", g.n)
                G.indirect_dma_start(out=q[:, g.buf2, k], out_offset=None, in_=table,
                                     in_offset=bass.IndirectOffsetOnAxis(ap=idx[:, g.buf2, k, 0:1], axis=0)
                                     ).then_inc(gath[g.buf4], 16)

            def products(g):
                need(pool, gath[g.buf4], 16 * NT * (g.quarter + 1))
                need(pool, b_red, g.n)
                G.tensor_tensor(prod[:], q[:, g.buf2, :, 2 * D:3 * D], Y[:, g.buf4], ALU.mult).then_inc(b_p, 1)

            def finish(g):
                need(pool, b_pr, g.n + 1)
                xg = X[:, g.buf4].rearrange("p (k d) -> p k d", d=D)
                G.tensor_tensor(xg, xg, q[:, g.buf2, :, 0:D], ALU.add).then_inc(b_fin, 1)

            def body_b(i):
                for r in range(U):
                    g, before = Group(i, r), Group(i, r - 1)
                    one, two = Group(i, r + 1), Group(i, r + 2)
                    for k in range(NT):
                        gather(g, k)
                        if before.exists():
                            if k == 1:
                                products(before)
                            if k == 8:
                                finish(before)
                        if one.exists() and k == 4:
                            low_half(one)
                        if two.exists() and k == 12:
                            inverse_deviation(two)

            pool.wait_ge(tab_out, 16)
            inverse_deviation(Group(0, 0))
            low_half(Group(0, 0))
            inverse_deviation(Group(0, 1))
            body_b(0)
            with pool.Fori(1, NI - 1) as i:
                body_b(i)
            body_b(NI - 1)
            products(Group(NI - 1, U - 1))
            finish(Group(NI - 1, U - 1))


def shape_constants():
    def cosines(freq, pos, n, weight_of):
        ends = (weight_of == 0) | (weight_of == n - 1)
        return np.cos(np.pi * np.multiply.outer(pos, freq) / (n - 1)) * np.where(ends, 1.0, 2.0)

    kx = np.concatenate([np.arange(MX // 2), np.arange(H - MX // 2, H)])
    ky = np.arange(MY)
    h, w = np.arange(H), np.arange(W)
    fh = cosines(kx, h, H, h[:, None]).reshape(P, T2, MX)
    fw = cosines(ky, w, W, w[:, None]).reshape(2, P, MY).transpose(1, 0, 2)
    ih = cosines(kx, h, H, kx[None, :]).reshape(P, T2, MX).transpose(2, 1, 0).reshape(MX, T2 * P)
    iw = np.tile(cosines(ky, w, W, ky[None, :]).T, (CG, 1))
    gm = (np.arange(P)[:, None] % C) // CG == np.arange(C // CG)[None, :]
    rm = np.arange(P)[:, None] == D + np.arange(3)[None, :]
    return [np.ascontiguousarray(a, dtype=np.float32) for a in (fh, fw, ih, iw, np.eye(P), gm, rm)]


def kernel(x, L0_conv_weights1, L0_conv_weights2, L1_conv_embeddings):
    import concourse.bacc as bacc
    from concourse.bass_utils import run_bass_kernel_spmd

    nc = bacc.Bacc("TRN2", target_bir_lowering=False, num_devices=1)
    given = [x, L0_conv_weights1, L0_conv_weights2, L1_conv_embeddings] + shape_constants()
    names = ["x", "w1", "w2", "emb", "c_fh", "c_fw", "c_ih", "c_iw", "c_id", "c_gm", "c_rm"]
    arrays = {n: np.ascontiguousarray(a) for n, a in zip(names, given)}
    args = [nc.dram_tensor(n, a.shape, F32, kind="ExternalInput").ap() for n, a in arrays.items()]
    args.append(nc.dram_tensor("y", (B, C, H, W), F32, kind="ExternalOutput").ap())
    program(nc, *args)
    return run_bass_kernel_spmd(nc, [arrays], core_ids=[0]).results[0]["y"]
```

```python
from contextlib import ExitStack

import numpy as np

import concourse.bass as bass
from concourse import mybir

ALU = mybir.AluOpType
ACT = mybir.ActivationFunctionType
AX_X = mybir.AxisListType.X
F32 = mybir.dt.float32
F16 = mybir.dt.float16
I32 = mybir.dt.int32
U32 = mybir.dt.uint32
RMAX = bass.bass_isa.ReduceOp.max

P = 128
B, C, H, W = 8, 64, 256, 256
CG = 2
NG = B * C // CG
U = 8
NI = NG // U
T2 = H // P
MX, MY = 64, 32
HALF = MX // 2 * MY
CH = 128
NCH = HALF // CH
KX = CH // MY
CB = 512 // C
NB = MY // CB
WI = 16
WO = C // WI
D = 64
K = 1024
NP = K // 2
NT = CG * H * W // D // P
PT = 7
ROW = 3 * D + 4
DC = float((2 * (H - 1)) * (2 * (W - 1)))
EPS = 1e-5
E_SCALE = 2.0 ** 14
Y_SCALE = 2.0 ** 7
ONE = 2.0 ** 15


class Group:

    def __init__(self, i, r):
        self.i, self.r = i, r
        self.n = U * i + r
        self.buf8, self.buf4, self.buf2 = r % 8, r % 4, r % 2

    def visit(self, size):
        return U // size * self.i + self.r // size

    def exists(self):
        return not isinstance(self.n, int) or 0 <= self.n < NG


def need(eng, sem, count):
    if not isinstance(count, int) or count > 0:
        eng.wait_ge(sem, count)


def program(nc, x, w1, w2, emb, c_fh, c_fw, c_ih, c_iw, c_id, c_gm, c_rm, out):
    spec = nc.dram_tensor("spec", [B, C, MX * MY], F32, kind="Internal").ap()
    mixed = nc.dram_tensor("mixed", [NG, MX, CG * MY], F32, kind="Internal").ap()
    table = nc.dram_tensor("table", [NP, ROW], F32, kind="Internal").ap()

    x_g = x.rearrange("b (g i) (p t) w -> (b g) p i (t w)", i=CG, t=T2)
    out_g = out.rearrange("b (g i) (p t) w -> (b g) p i (t w)", i=CG, t=T2)
    spec_g = spec.rearrange("b (g i) (x y) -> (b g) (i x) y", i=CG, y=MY)
    spec_c = spec.rearrange("b c m -> c b m")
    mixed_b = mixed.rearrange("(b g) x f -> b g x f", b=B)
    w_m = [w.rearrange("i o x y -> i o (x y)") for w in (w1, w2)]

    with ExitStack() as ctx:
        def sb(name, shape, dt=F32):
            return ctx.enter_context(nc.sbuf_tensor(name, shape, dt))

        def sem(name):
            return ctx.enter_context(nc.semaphore(name))

        bank = [ctx.enter_context(nc.psum_tensor(f"bank{n}", [P, 512], F32)) for n in range(8)]

        fh = sb("fh", [P, T2, MX])
        fw = sb("fw", [P, 2, MY])
        ih = sb("ih", [MX, T2 * P])
        iw = sb("iw", [CG * MY, W])
        ident = sb("ident", [P, P])
        gmask = sb("gmask", [P, C // CG])
        rmask = sb("rmask", [P, 3])
        ident16 = sb("ident16", [P, P], F16)
        avg = sb("avg", [P, P])
        ones = sb("ones", [D, P])
        mhalf = sb("mhalf", [P, B])
        avg_all = sb("avg_all", [P, P])
        consts = ((fh, c_fh), (fw, c_fw), (ih, c_ih), (iw, c_iw), (ident, c_id), (gmask, c_gm), (rmask, c_rm))

        E = sb("E", [P, NP, 2])
        S = sb("S", [P, 2, NP])
        S2 = sb("S2", [P, 2, NP])
        eh = sb("eh", [P, 2, NP], F16)
        el = sb("el", [P, 2, NP], F16)
        part = sb("part", [P, 2, NP], F16)
        tb = sb("tb", [P, 4, ROW])
        tsq = sb("tsq", [P, 4, 2, D])
        tnorm = sb("tnorm", [P, 4, 2])
        sc = sb("sc", [P, 9])
        amax0, amax, inv_a, inv_s, ymul, ymulh, bscale, escale, ymuln = (sc[:, n:n + 1] for n in range(9))

        X = sb("X", [P, 8, CG * T2 * W])        
        st = sb("st", [P, U, 2, 6])
        mvs = sb("mvs", [P, U, 2])
        mv_all = sb("mv_all", [P, NG, 2])
        dev_all = sb("dev_all", [P, NG])
        mean_all = sb("mean_all", [P, NG])
        sel8 = sb("sel8", [P, B, C // CG])
        v_c = sb("v_c", [P, B])
        r_c = sb("r_c", [P, B])
        m_c = sb("m_c", [P, B])
        dc_fix = sb("dc_fix", [C, B])
        Us = sb("Us", [MX, 2, 512])
        UTs = sb("UTs", [P, 2, 256])
        Fs = sb("Fs", [P, 8, MY])
        arena = sb("arena", [P, 2 * C * CH])
        Wc = arena[:].rearrange("p (v o m) -> p v o m", v=2, o=C)
        taken = [0]

        def from_arena(*dims):
            size = int(np.prod(dims))
            taken[0] += size
            assert taken[0] <= 2 * C * CH
            names = "abc"[:len(dims)]
            return arena[:, taken[0] - size:taken[0]].rearrange(
                f"p ({' '.join(names)}) -> p {' '.join(names)}", **dict(zip(names, dims)))

        Xc = sb("Xc", [P, 2, B, CH])
        Xb = sb("Xb", [P, 2, CH, 2 * B])
        Oc = sb("Oc", [P, 2, C, MY])
        M = sb("M", [MX, 2, CG * MY])
        Ts = sb("Ts", [CG * MY, T2 * P])
        sums = sb("sums", [P, 3])
        squares = sb("squares", [P, CG * T2 * W], F16)
        small = sb("small", [P, 8])
        mean1, delta2, ve, rs, rr, rrn, nb = (small[:, n:n + 1] for n in range(7))
        YS = sb("YS", [P, NT, 2 * D], F16)
        Y = from_arena(4, NT, D)
        t1 = sb("t1", [P, 2, NT, P], F16)
        t2 = sb("t2", [P, 2, NT, P], F16)
        R = from_arena(4, NP)
        Fm = from_arena(4, NP)
        mx = sb("mx", [P, 4])
        idx = sb("idx", [P, 2, NT, 8], U32)
        q = from_arena(2, NT, ROW)
        prod = from_arena(PT, D)
        prodv = from_arena(NT - PT, D)
        dot = sb("dot", [P, NT])
        odd = sb("odd", [P, NT], I32)

        consts_in = sem("consts_in")
        emb_in = sem("emb_in")
        held = {n: sem(f"held_{n}") for n in ("pe", "act", "dve", "pool")}
        dve_step = sem("dve_step")
        ids_ready = sem("ids_ready")
        amax_in = sem("amax_in")
        amax_all = sem("amax_all")
        esq_in = sem("esq_in")
        esq_done = sem("esq_done")
        tab_tr = sem("tab_tr")
        tab_ready = sem("tab_ready")
        tab_out = sem("tab_out")
        codes_ready = sem("codes_ready")

        xa_in = [sem(f"xa_in{n}") for n in range(U)]
        a_h, a_u, a_tr, a_ut, a_w, a_f = (sem(n) for n in ("a_h", "a_u", "a_tr", "a_ut", "a_w", "a_f"))
        a_bn, a_mv, a_mvc = (sem(n) for n in ("a_bn", "a_mv", "a_mvc"))
        fs_out = [sem(f"fs_out{n}") for n in range(8)]
        s_mean, s_dev, s_var, s_ve, s_rstd = (sem(n) for n in ("s_mean", "s_dev", "s_var", "s_ve", "s_rstd"))
        w_in = [sem(f"w_in{n}") for n in range(2)]
        xs_in = [sem(f"xs_in{n}") for n in range(2)]
        m_x, m_mm, m_ev = (sem(n) for n in ("m_x", "m_mm", "m_ev"))
        o_out = [sem(f"o_out{n}") for n in range(2)]

        x_in = [sem(f"x_in{n}") for n in range(8)]
        m_in = [sem(f"m_in{n}") for n in range(2)]
        y_out = [sem(f"y_out{n}") for n in range(8)]
        gath = [sem(f"gath{n}") for n in range(4)]
        b_inv, b_t, b_conv, b_x1, b_sq, b_st, b_mean, b_delta2, b_ve, b_rs, b_rr, b_nb = (
            sem("b_" + n) for n in "inv t conv x1 sq st mean delta2 ve rs rr nb".split())
        b_y, b_yl, b_tp, b_te, b_sc, b_rl, b_ttr, b_mi, b_p, b_dot, b_red, b_sel, b_pr, b_fin = (
            sem("b_" + n) for n in "y yl tp te sc rl ttr mi p dot red sel pr fin".split())

        def hold(eng, name, count):
            if not isinstance(count, int):
                eng.sem_inc(held[name], 1)

        block = ctx.enter_context(nc.Block())

        @block.sync
        def _(sp):
            sp.dma_start(E[0:D], emb.rearrange("d (j e) -> d j e", e=2)).then_inc(emb_in, 16)
            sp.dma_start(E[D:P], emb.rearrange("d (j e) -> d j e", e=2)).then_inc(emb_in, 16)
            for tile, src in consts:
                sp.dma_start(tile[:], src).then_inc(consts_in, 16)

            def load_weights(c, v, outs=slice(0, C)):
                for n in range(2):
                    sp.dma_start(Wc[64 * n:64 * n + 64, v, outs],
                                 w_m[n][:, outs, bass.ds(c * CH, CH)]).then_inc(w_in[v], 16)

            def group_a(g):
                need(sp, a_h, g.n - 7)
                need(sp, a_bn, g.n - 7)
                sp.dma_start(X[:, g.buf8].rearrange("p (i f) -> p i f", i=CG), x_g[g.n]).then_inc(xa_in[g.buf8], 16)

            def store_a(g):
                need(sp, a_f, g.n + 1)
                sp.dma_start(spec_g[g.n], Fs[:, g.buf8]).then_inc(fs_out[g.buf8], 16)

            def body_a(i):
                for r in range(U):
                    group_a(Group(i, r))
                    if Group(i, r - 6).exists():
                        store_a(Group(i, r - 6))

            body_a(0)
            with sp.Fori(1, WI + 1) as i:
                body_a(i)
                for v in range(2):
                    load_weights(v, v, bass.ds((i - 1) * WO, WO))
            with sp.Fori(WI + 1, NI) as i:
                body_a(i)
            for r in range(2, U):
                store_a(Group(NI - 1, r))
            sp.wait_ge(tab_ready, 1)
            sp.dma_start(table.rearrange("(c p) w -> p c w", p=P), tb[:]).then_inc(tab_out, 16)
            for n in range(8):
                sp.wait_ge(fs_out[n], 16 * NI)

            def load_m(i, v):
                c = 2 * i + v
                need(sp, m_x, c - 1)
                for n in range(2):
                    sp.dma_start(Xc[64 * n:64 * n + 64, v],
                                 spec_c[:, :, bass.ds(c * CH + n * HALF, CH)]).then_inc(xs_in[v], 16)
                if not (isinstance(i, int) and i == 0):
                    need(sp, m_mm, NB * (c - 1))
                    load_weights(c, v)

            load_m(0, 0)
            load_m(0, 1)
            with sp.Fori(1, NCH // 2) as i:
                for v in range(2):
                    load_m(i, v)

            def load_x(g):
                need(sp, y_out[g.buf8], 16 * g.visit(8))
                sp.dma_start(X[:, g.buf8].rearrange("p (i f) -> p i f", i=CG), x_g[g.n]).then_inc(x_in[g.buf8], 16)

            def load_modes(g):
                need(sp, b_inv, g.n - 1)
                sp.dma_start(M[:, g.buf2], mixed[g.n]).then_inc(m_in[g.buf2], 16)

            def store_y(g):
                need(sp, b_fin, g.n + 1)
                sp.dma_start(out_g[g.n], X[:, g.buf8].rearrange("p (i f) -> p i f", i=CG)).then_inc(y_out[g.buf8], 16)

            sp.wait_ge(a_h, NG)
            sp.wait_ge(a_bn, NG)
            for r in range(5):
                load_x(Group(0, r))
            for n in range(2):
                sp.wait_ge(o_out[n], 32 * KX * (NCH // 2))
            for r in range(3):
                load_modes(Group(0, r))

            def body(i):
                for r in range(U):
                    if Group(i, r + 3).exists():
                        load_modes(Group(i, r + 3))
                    if Group(i, r - 1).exists():
                        store_y(Group(i, r - 1))
                    if Group(i, r + 5).exists():
                        load_x(Group(i, r + 5))

            body(0)
            with sp.Fori(1, NI - 1) as i:
                body(i)
            body(NI - 1)
            store_y(Group(NI - 1, U - 1))
            for n in range(U):
                sp.wait_ge(y_out[n], 16 * NI)

        @block.tensor
        def _(pe):
            pe.wait_ge(consts_in, 16 * len(consts))
            pe.wait_ge(ids_ready, 1)

            pe.wait_ge(esq_in, 1)
            for e in range(2):
                last = nc.tensor.matmul(bank[e][:], ones[:], S2[0:D, e], start=True, stop=True)
            last.then_inc(esq_done, 1)
            for c in range(4):
                for e in range(2):
                    last = nc.tensor.transpose(bank[2][:, (2 * c + e) * D:(2 * c + e + 1) * D],
                                               E[0:D, c * P:(c + 1) * P, e], ident[0:D, 0:D])
            last.then_inc(tab_tr, 1)
            pe.wait_ge(codes_ready, 1)

            def dct_h(g):
                need(pe, xa_in[g.buf8], 16 * (g.visit(8) + 1))
                need(pe, a_u, g.n - 1)
                xg = X[:, g.buf8].rearrange("p (i t w) -> p t i w", i=CG, t=T2)
                for t in range(T2):
                    last = nc.tensor.matmul(bank[g.buf2][0:MX], fh[:, t], xg[:, t], start=t == 0, stop=t == T2 - 1)
                last.then_inc(a_h, 1)

            def turn(g):
                need(pe, a_u, g.n + 1)
                need(pe, a_ut, g.n - 1)
                hold(pe, "pe", g.n)
                for wc in range(2):
                    for i in range(CG):
                        last = nc.tensor.transpose(bank[2 + g.buf2][:, (2 * wc + i) * MX:(2 * wc + i + 1) * MX],
                                                   Us[:, g.buf2, i * W + wc * P:i * W + (wc + 1) * P],
                                                   ident[0:MX, 0:MX])
                last.then_inc(a_tr, 1)

            def dct_w(g):
                need(pe, a_ut, g.n + 1)
                need(pe, a_f, g.n - 1)
                for wc in range(2):
                    last = nc.tensor.matmul(bank[4 + g.buf2][:, 0:MY], UTs[:, g.buf2, wc * P:(wc + 1) * P],
                                            fw[:, wc], start=wc == 0, stop=wc == 1)
                last.then_inc(a_w, 1)

            def body_a(i):
                for r in range(U):
                    dct_h(Group(i, r))
                    if Group(i, r - 2).exists():
                        dct_w(Group(i, r - 2))
                    if Group(i, r - 1).exists():
                        turn(Group(i, r - 1))

            body_a(0)
            with pe.Fori(1, NI) as i:
                body_a(i)
            dct_w(Group(NI - 1, U - 2))
            turn(Group(NI - 1, U - 1))
            dct_w(Group(NI - 1, U - 1))

            pe.wait_ge(a_mvc, NI)
            nc.tensor.matmul(bank[6][:, 0:NG], avg[:], mv_all[:, :, 0], start=True, stop=True).then_inc(s_mean, 1)
            pe.wait_ge(s_dev, 1)
            nc.tensor.matmul(bank[7][:, 0:NG], avg[:], dev_all[:], start=True, stop=True).then_inc(s_var, 1)

            pe.wait_ge(a_ut, NG)
            pe.wait_ge(a_f, NG)

            def mix(i, v):
                c = 2 * i + v
                need(pe, w_in[v], 32 * (WI + i))
                need(pe, m_x, c + 1)
                for bk in range(NB):
                    need(pe, m_ev, NB * (c - 2) + bk + 1)
                    hold(pe, "pe", i)
                    for j in range(KX):
                        for n in range(CB):
                            m = j * MY + bk * CB + n
                            last = nc.tensor.matmul(bank[NB * v + bk][32 * j:32 * j + 2 * B, n * C:(n + 1) * C],
                                                    Xb[:, v, m], Wc[:, v, :, m], start=True, stop=True,
                                                    tile_position=(0, 32 * j))
                    last.then_inc(m_mm, 1)

            mix(0, 0)
            mix(0, 1)
            with pe.Fori(1, NCH // 2) as i:
                for v in range(2):
                    mix(i, v)

            pe.wait_ge(m_ev, NB * NCH)
            tp = bank[7][:].bitcast(F16).rearrange("p (k f) -> p k f", k=NT // 2)

            def inverse_h(g):
                need(pe, m_in[g.buf2], 16 * (g.visit(2) + 1))
                need(pe, b_ve, g.n)
                hold(pe, "pe", g.n)
                nc.tensor.matmul(bank[6][0:CG * MY, 0:T2 * P], M[:, g.buf2], ih[:], start=True,
                                 stop=True).then_inc(b_inv, 1)

            def inverse_w(g, i):
                need(pe, x_in[g.buf8], 16 * (g.visit(8) + 1))
                need(pe, b_t, g.n + 1)
                need(pe, b_x1, 2 * g.n + i)
                nc.tensor.matmul(bank[6][:], ident[:], X[:, g.buf8, 512 * i:512 * (i + 1)], start=True, stop=False)
                rows = slice(i * MY, (i + 1) * MY)
                for t in range(T2):
                    last = nc.tensor.matmul(bank[6][:, t * W:(t + 1) * W], Ts[rows, t * P:(t + 1) * P],
                                            iw[rows], start=False, stop=t == T2 - 1)
                last.then_inc(b_conv, 1)

            def statistics(g):
                need(pe, b_sq, g.n + 1)
                nc.tensor.matmul(bank[6][:, 0:3], avg_all[:], sums[:], start=True, stop=True).then_inc(b_st, 1)

            def turn_y(g, half):
                need(pe, b_yl, g.n + 1)
                need(pe, b_te, 2 * g.n + half)
                for k in range(NT // 2):
                    last = nc.tensor.transpose(tp[:, k], YS[:, half * (NT // 2) + k], ident16[:])
                last.then_inc(b_tp, 1)

            def scores(g, k):
                n = NT * g.n + k
                if k % (NT // 2) == 0:
                    need(pe, b_te, 2 * g.n + 1 + k // (NT // 2))
                need(pe, b_ttr, n - 3)
                need(pe, b_rl, n - 1)
                for rows, tile, codes in ((P, t1, eh), (D + 3, t2, el)):
                    for e in range(2):
                        last = nc.tensor.matmul(bank[4 + k % 2 if e else k % 4][:], tile[0:rows, g.buf2, k],
                                                codes[0:rows, e], start=rows == P, stop=rows != P)
                last.then_inc(b_sc, 1)

            def body_b(i):
                for r in range(U):
                    g, one, two = Group(i, r), Group(i, r + 1), Group(i, r + 2)
                    for k in range(NT):
                        scores(g, k)
                        if two.exists():
                            if k == 0:
                                inverse_h(two)
                            if k == 3:
                                inverse_w(two, 0)
                            if k == 5:
                                inverse_w(two, 1)
                            if k == 9:
                                statistics(two)
                        if one.exists():
                            if k == 12:
                                turn_y(one, 0)
                            if k == 15:
                                turn_y(one, 1)

            for r in range(2):
                inverse_h(Group(0, r))
                inverse_w(Group(0, r), 0)
                inverse_w(Group(0, r), 1)
                statistics(Group(0, r))
            turn_y(Group(0, 0), 0)
            turn_y(Group(0, 0), 1)
            body_b(0)
            with pe.Fori(1, NI - 1) as i:
                body_b(i)
            body_b(NI - 1)

        @block.scalar
        def _(act):
            def take_u(g):
                need(act, a_h, g.n + 1)
                need(act, a_tr, g.n - 1)
                nc.scalar.copy(Us[:, g.buf2], bank[g.buf2][0:MX]).then_inc(a_u, 1)

            def take_f(g):
                need(act, a_w, g.n + 1)
                need(act, fs_out[g.buf8], 16 * g.visit(8))
                nc.scalar.copy(Fs[:, g.buf8], bank[4 + g.buf2][:, 0:MY]).then_inc(a_f, 1)

            def body_a(i):
                for r in range(U):
                    take_u(Group(i, r))
                    if Group(i, r - 2).exists():
                        take_f(Group(i, r - 2))

            body_a(0)
            with act.Fori(1, NI) as i:
                body_a(i)
            take_f(Group(NI - 1, U - 2))
            take_f(Group(NI - 1, U - 1))

            def take_mix(i, v):
                c = 2 * i + v
                need(act, o_out[v], 32 * KX * i)
                for bk in range(NB):
                    need(act, m_mm, NB * c + bk + 1)
                    for j in range(KX):
                        rows = slice(32 * j, 32 * j + 2 * B)
                        last = nc.scalar.copy(Oc[rows, v, :, CB * bk:CB * (bk + 1)].rearrange("p o m -> p m o"),
                                              bank[NB * v + bk][rows].rearrange("p (m o) -> p m o", m=CB))
                    last.then_inc(m_ev, 1)
                act.wait_ge(m_ev, NB * (c + 1))
                for n in range(2):
                    for j in range(KX):
                        act.dma_start(mixed_b[:, :, bass.ds(c * KX + j + n * MX // 2, 1)],
                                      Oc[32 * j + n * B:32 * j + (n + 1) * B, v].rearrange(
                                          "b (g i) y -> b g (i y)", i=CG).unsqueeze(2)).then_inc(o_out[v], 16)

            take_mix(0, 0)
            take_mix(0, 1)
            with act.Fori(1, NCH // 2) as i:
                for v in range(2):
                    take_mix(i, v)

            tp = bank[7][:].bitcast(F16).rearrange("p (k f) -> p k f", k=NT // 2)

            def take_t(g):
                need(act, b_inv, g.n + 1)
                need(act, b_conv, 2 * g.n)
                nc.scalar.copy(Ts[:], bank[6][0:CG * MY, 0:T2 * P]).then_inc(b_t, 1)

            def take_x(g, i):
                need(act, b_conv, 2 * g.n + i + 1)
                need(act, b_st, g.n)
                nc.scalar.activation(X[:, g.buf8, 512 * i:512 * (i + 1)], bank[6][:], ACT.Identity,
                                     accum_out=sums[:, i:i + 1]).then_inc(b_x1, 1)

            def square_sum(g):
                need(act, b_x1, 2 * g.n + 2)
                nc.scalar.activation(squares[:], X[:, g.buf8], ACT.Square, scale=-1.0,
                                     bias=mean_all[:, bass.ds(g.n, 1)], accum_out=sums[:, 2:3]).then_inc(b_sq, 1)

            def delta2_of(g):
                need(act, b_mean, g.n + 1)
                need(act, b_ve, g.n)
                hold(act, "act", g.n)
                nc.scalar.activation(delta2, mean1, ACT.Square, scale=-1.0,
                                     bias=mean_all[:, bass.ds(g.n, 1)]).then_inc(b_delta2, 1)

            def scale_of(g):
                need(act, b_rs, g.n + 1)
                need(act, b_y, g.n)
                nc.scalar.activation(rr, rs, ACT.Identity, scale=ymul)
                nc.scalar.activation(rrn, rs, ACT.Identity, scale=ymuln).then_inc(b_rr, 1)

            def bias_of(g):
                need(act, b_rr, g.n + 1)
                nc.scalar.activation(nb, mean1, ACT.Identity, scale=rrn).then_inc(b_nb, 1)

            def high_half(g):
                need(act, b_nb, g.n + 1)
                need(act, b_tp, 2 * g.n)
                xg = X[:, g.buf8].rearrange("p (k d) -> p k d", d=D)
                nc.scalar.activation(YS[:, :, 0:D], xg, ACT.Identity, bias=nb, scale=rr)

            def normalise(g):
                need(act, b_p, g.n - 3)
                need(act, b_dot, g.n - 3)
                xg = X[:, g.buf8].rearrange("p (k d) -> p k d", d=D)
                nc.scalar.activation(Y[:, g.buf4], xg, ACT.Identity, bias=nb, scale=rr).then_inc(b_y, 1)

            def take_y(g, half):
                need(act, b_tp, 2 * g.n + half + 1)
                need(act, b_sc, NT * (g.n - 1))
                ks = slice(half * (NT // 2), (half + 1) * (NT // 2))
                nc.scalar.copy(t1[:, g.buf2, ks], tp)
                nc.scalar.copy(t2[0:D, g.buf2, ks], tp[0:D]).then_inc(b_te, 1)

            def relu(g, k):
                n = NT * g.n + k
                need(act, b_sc, n + 1)
                need(act, b_ttr, n - 3)
                nc.scalar.activation(R[:, k % 4], bank[4 + k % 2][:], ACT.Relu).then_inc(b_rl, 1)

            def body_b(i):
                for r in range(U):
                    g, one, two = Group(i, r), Group(i, r + 1), Group(i, r + 2)
                    for k in range(NT):
                        relu(g, k)
                        if one.exists():
                            if k == 3:
                                scale_of(one)
                            if k == 4:
                                bias_of(one)
                            if k == 7:
                                high_half(one)
                            if k == 8:
                                normalise(one)
                            if k == 13:
                                take_y(one, 0)
                            if k == 15:
                                take_y(one, 1)
                        if two.exists():
                            if k == 1:
                                take_t(two)
                            if k == 3:
                                take_x(two, 0)
                            if k == 5:
                                take_x(two, 1)
                            if k == 6:
                                square_sum(two)
                            if k == 13:
                                delta2_of(two)

            act.wait_ge(codes_ready, 1)
            for r in range(2):
                take_t(Group(0, r))
                take_x(Group(0, r), 0)
                take_x(Group(0, r), 1)
                square_sum(Group(0, r))
                delta2_of(Group(0, r))
                if r == 0:
                    scale_of(Group(0, 0))
                    bias_of(Group(0, 0))
                    high_half(Group(0, 0))
                    normalise(Group(0, 0))
            take_y(Group(0, 0), 0)
            take_y(Group(0, 0), 1)
            body_b(0)
            with act.Fori(1, NI - 1) as i:
                body_b(i)
            body_b(NI - 1)

        @block.vector
        def _(dve):
            steps = [0]

            def then(ins):
                steps[0] += 1
                ins.then_inc(dve_step, 1)
                dve.wait_ge(dve_step, steps[0])

            V = nc.vector
            V.memset(avg[:], 1.0 / P)
            V.memset(avg_all[:], 1.0 / (P * CG * T2 * W))
            V.memset(ones[:], 1.0)
            V.memset(mhalf[:], -0.5)
            V.memset(t2[D:P], ONE)
            V.memset(Xb[:], 0.0)
            V.memset(tb[:], 0.0)
            dve.wait_ge(consts_in, 16 * len(consts))
            V.tensor_copy(ident16[:], ident[:]).then_inc(ids_ready, 1)

            dve.wait_ge(emb_in, 32)
            Ef = E[:].rearrange("p j e -> p (j e)")
            V.tensor_reduce(amax0, Ef, AX_X, ALU.max, apply_absolute_value=True).then_inc(amax_in, 1)
            V.tensor_tensor(S2[:].rearrange("p e j -> p j e"), E[:], E[:], ALU.mult).then_inc(esq_in, 1)
            dve.wait_ge(amax_all, 1)
            then(V.tensor_scalar(amax, amax, 1e-30, None, ALU.max))
            then(V.reciprocal(inv_a, amax))
            then(V.tensor_scalar(inv_s, amax, 1.0 / 16.0, 1.0, ALU.mult, ALU.max))
            then(V.reciprocal(inv_s, inv_s))
            V.tensor_scalar(ymul, inv_s, Y_SCALE, None, ALU.mult)
            V.tensor_scalar(ymuln, inv_s, -Y_SCALE, None, ALU.mult)
            V.tensor_scalar(ymulh, inv_s, Y_SCALE / 2, None, ALU.mult)
            V.tensor_scalar(escale, inv_a, E_SCALE, None, ALU.mult)
            then(V.scalar_tensor_tensor(bscale, inv_a, -Y_SCALE * E_SCALE / 2 / ONE, inv_s, ALU.mult, ALU.mult))
            then(V.tensor_tensor(S[:, 1], E[:, :, 1], E[:, :, 0], ALU.subtract))
            V.tensor_scalar(S[:, 0], E[:, :, 0], escale, None, ALU.mult)
            then(V.tensor_scalar(S[:, 1], S[:, 1], escale, None, ALU.mult))
            then(V.tensor_copy(eh[:], S[:]))
            then(V.tensor_tensor(el[0:D], S[0:D], eh[0:D], ALU.subtract))
            dve.wait_ge(esq_done, 1)
            then(V.tensor_copy(S[:, 0], bank[0][:]))
            then(V.tensor_tensor(S[:, 1], bank[1][:], S[:, 0], ALU.subtract))
            then(V.tensor_scalar(S[:], S[:], bscale, None, ALU.mult))
            for n in range(3):
                then(V.tensor_copy(part[:], S[:]))
                if n == 0:
                    then(V.tensor_scalar(el[D:P], part[D:P], rmask[D:P, 0:1], None, ALU.mult))
                else:
                    then(V.scalar_tensor_tensor(el[D:P], part[D:P], rmask[D:P, n:n + 1], el[D:P], ALU.mult, ALU.add))
                if n < 2:
                    then(V.tensor_tensor(S[:], S[:], part[:], ALU.subtract))
            dve.wait_ge(tab_tr, 1)
            tt = bank[2][:].rearrange("p (c e d) -> p c e d", c=4, e=2)
            V.tensor_copy(tb[:, :, 0:D], tt[:, :, 0])
            then(V.tensor_copy(tb[:, :, D:2 * D], tt[:, :, 1]))
            V.tensor_tensor(tb[:, :, 2 * D:3 * D], tb[:, :, D:2 * D], tb[:, :, 0:D], ALU.subtract)
            te = tb[:, :, 0:2 * D].rearrange("p c (e d) -> p c e d", e=2)
            then(V.tensor_tensor(tsq[:], te, te, ALU.mult))
            then(V.tensor_reduce(tnorm[:], tsq[:], AX_X, ALU.add))
            then(V.tensor_tensor(tnorm[:, :, 0], tnorm[:, :, 1], tnorm[:, :, 0], ALU.subtract))
            then(V.tensor_scalar(tb[:, :, 3 * D], tnorm[:, :, 0], ymulh, None, ALU.mult))
            dve.sem_inc(tab_ready, 1)
            dve.sem_inc(codes_ready, 2)

            def stats(g):
                need(dve, xa_in[g.buf8], 16 * (g.visit(8) + 1))
                for n in range(2):
                    last = V.bn_stats(st[:, g.buf8, n], X[:, g.buf8, 512 * n:512 * (n + 1)])
                last.then_inc(a_bn, 1)

            def join(g):
                need(dve, a_bn, g.n + 1)
                need(dve, a_mvc, g.visit(8))
                hold(dve, "dve", g.n)
                V.bn_aggr(mvs[:, g.buf8], st[:, g.buf8]).then_inc(a_mv, 1)

            def take_ut(g):
                need(dve, a_tr, g.n + 1)
                need(dve, a_w, g.n - 1)
                V.tensor_copy(UTs[:, g.buf2], bank[2 + g.buf2][:, 0:256]).then_inc(a_ut, 1)

            def body_a(i):
                for r in range(U):
                    stats(Group(i, r))
                    if Group(i, r - 1).exists():
                        take_ut(Group(i, r - 1))
                    join(Group(i, r))
                need(dve, a_mv, U * (i + 1))
                V.tensor_copy(mv_all[:, bass.ds(U * i, U), :], mvs[:]).then_inc(a_mvc, 1)

            body_a(0)
            with dve.Fori(1, NI) as i:
                body_a(i)
            take_ut(Group(NI - 1, U - 1))

            dve.wait_ge(s_mean, 1)
            then(V.tensor_copy(mean_all[:], bank[6][:, 0:NG]))
            then(V.tensor_tensor(dev_all[:], mv_all[:, :, 0], mean_all[:], ALU.subtract))
            then(V.tensor_tensor(dev_all[:], dev_all[:], dev_all[:], ALU.mult))
            V.tensor_tensor(dev_all[:], dev_all[:], mv_all[:, :, 1], ALU.add).then_inc(s_dev, 1)
            gm = gmask[:].unsqueeze(1).broadcast_to([P, B, C // CG])
            then(V.tensor_tensor(sel8[:], mean_all[:].rearrange("p (b g) -> p b g", b=B), gm, ALU.mult))
            then(V.tensor_reduce(m_c[:], sel8[:], AX_X, ALU.add))
            dve.wait_ge(s_var, 1)
            then(V.tensor_tensor(sel8[:], bank[7][:, 0:NG].rearrange("p (b g) -> p b g", b=B), gm, ALU.mult))
            then(V.tensor_reduce(v_c[:], sel8[:], AX_X, ALU.add))
            V.tensor_scalar(v_c[:], v_c[:], EPS, None, ALU.add).then_inc(s_ve, 1)
            dve.wait_ge(s_rstd, 1)
            then(V.scalar_tensor_tensor(dc_fix[:], m_c[0:C], DC, r_c[0:C], ALU.mult, ALU.mult))

            def scale(i, v):
                c = 2 * i + v
                need(dve, xs_in[v], 32 * (i + 1))
                need(dve, m_mm, NB * (c - 1))
                for n in range(2):
                    half = slice(64 * n, 64 * n + 64)
                    last = V.tensor_tensor(Xb[half, v, :, n * B:(n + 1) * B],
                                           Xc[half, v].rearrange("p b m -> p m b"),
                                           r_c[half].unsqueeze(1).broadcast_to([64, CH, B]), ALU.mult)
                if isinstance(i, int) and c == 0:
                    then(last)
                    last = V.tensor_tensor(Xb[0:C, v, 0, 0:B], Xb[0:C, v, 0, 0:B], dc_fix[:], ALU.subtract)
                last.then_inc(m_x, 1)

            scale(0, 0)
            scale(0, 1)
            with dve.Fori(1, NCH // 2) as i:
                for v in range(2):
                    scale(i, v)

            def mean_of(g):
                need(dve, b_st, g.n + 1)
                need(dve, b_nb, g.n)
                V.tensor_reduce(mean1, bank[6][:, 0:2], AX_X, ALU.add).then_inc(b_mean, 1)

            def variance_of(g):
                need(dve, b_delta2, g.n + 1)
                V.scalar_tensor_tensor(ve, bank[6][:, 2:3], EPS, delta2, ALU.add, ALU.subtract).then_inc(b_ve, 1)

            def best(g, k):
                n = NT * g.n + k
                need(dve, b_rl, n + 1)
                need(dve, b_mi, n - 3)
                need(dve, b_ttr, n)
                hold(dve, "dve", g.n)
                V.tensor_tensor_reduce(out=Fm[:, k % 4], in0=bank[k % 4][:], in1=R[:, k % 4], scale=1.0,
                                       scalar=-3.0e38, op0=ALU.add, op1=ALU.max,
                                       accum_out=mx[:, k % 4:k % 4 + 1]).then_inc(b_ttr, 1)

            def find(g, k):
                if k == 0:
                    two = Group(g.i, g.r - 2)
                    need(dve, gath[two.buf4], 16 * NT * (two.visit(4) + 1))
                    hold(dve, "dve", g.n)
                V.max_index(idx[:, g.buf2, k], mx[:, k % 4:k % 4 + 1].broadcast_to([P, 8]),
                            Fm[:, k % 4]).then_inc(b_mi, 1)

            def dot_of(g, n):
                k = PT + n
                if n == 0:
                    need(dve, gath[g.buf4], 16 * NT * (g.visit(4) + 1))
                    need(dve, b_sel, g.n)
                    hold(dve, "dve", g.n)
                ins = V.tensor_tensor_reduce(out=prodv[:, n], in0=q[:, g.buf2, k, 2 * D:3 * D], in1=Y[:, g.buf4, k],
                                             scale=1.0, scalar=0.0, op0=ALU.mult, op1=ALU.add,
                                             accum_out=dot[:, k:k + 1])
                if k == NT - 1:
                    ins.then_inc(b_dot, 1)

            def sum_products(g):
                need(dve, b_p, g.n + 1)
                V.tensor_reduce(dot[:, 0:PT], prod[:], AX_X, ALU.add).then_inc(b_red, 1)

            def choose(g):
                need(dve, b_red, g.n + 1)
                need(dve, b_dot, g.n + 1)
                V.tensor_tensor(odd[:], dot[:], q[:, g.buf2, :, 3 * D], ALU.is_gt).then_inc(b_sel, 1)

            def settle(g):
                need(dve, b_sel, g.n + 1)
                hold(dve, "dve", g.n)
                V.copy_predicated(q[:, g.buf2, :, 0:D], odd[:].unsqueeze(2).broadcast_to([P, NT, D]),
                                  q[:, g.buf2, :, D:2 * D]).then_inc(b_pr, 1)

            def small_step(g, k, at):
                before, two = Group(g.i, g.r - 1), Group(g.i, g.r + 2)
                slot = 2 * k + at
                if before.exists():
                    if 10 <= slot < 10 + NT - PT:
                        dot_of(before, slot - 10)
                    if slot == 10 + NT - PT:
                        sum_products(before)
                    if slot == 11 + NT - PT:
                        choose(before)
                    if slot == 12 + NT - PT:
                        settle(before)
                if two.exists():
                    if slot == 16:
                        mean_of(two)
                    if slot == 24:
                        variance_of(two)

            def body_b(i):
                for r in range(U):
                    g, before = Group(i, r), Group(i, r - 1)
                    for k in range(NT):
                        best(g, k)
                        small_step(g, k, 0)
                        if k > 0:
                            find(g, k - 1)
                        elif before.exists():
                            find(before, NT - 1)
                        small_step(g, k, 1)

            for r in range(2):
                mean_of(Group(0, r))
                variance_of(Group(0, r))
            body_b(0)
            with dve.Fori(1, NI - 1) as i:
                body_b(i)
            body_b(NI - 1)
            last = Group(NI - 1, U - 1)
            dve.wait_ge(b_ttr, NT * NG)
            find(last, NT - 1)
            for n in range(NT - PT):
                dot_of(last, n)
            sum_products(last)
            choose(last)
            settle(last)

        @block.gpsimd
        def _(pool):
            G = nc.gpsimd
            pool.wait_ge(amax_in, 1)
            G.partition_all_reduce(amax, amax0, P, RMAX).then_inc(amax_all, 1)
            pool.wait_ge(s_ve, 1)
            G.tensor_tensor(r_c[:], v_c[:], mhalf[:], ALU.pow).then_inc(s_rstd, 1)

            def inverse_deviation(g):
                need(pool, b_ve, g.n + 1)
                need(pool, b_rr, g.n)
                G.tensor_tensor(rs, ve, mhalf[:, 0:1], ALU.pow).then_inc(b_rs, 1)

            def low_half(g):
                need(pool, b_y, g.n + 1)
                G.tensor_tensor(YS[:, :, D:2 * D], Y[:, g.buf4], YS[:, :, 0:D], ALU.subtract).then_inc(b_yl, 1)

            def gather(g, k):
                need(pool, b_mi, NT * g.n + k + 1)
                if k == 0:
                    need(pool, b_fin, g.n - 1)
                hold(pool, "pool", g.n)
                G.indirect_dma_start(out=q[:, g.buf2, k], out_offset=None, in_=table,
                                     in_offset=bass.IndirectOffsetOnAxis(ap=idx[:, g.buf2, k, 0:1], axis=0)
                                     ).then_inc(gath[g.buf4], 16)

            def products(g):
                need(pool, gath[g.buf4], 16 * NT * (g.visit(4) + 1))
                need(pool, b_red, g.n)
                G.tensor_tensor(prod[:], q[:, g.buf2, 0:PT, 2 * D:3 * D], Y[:, g.buf4, 0:PT], ALU.mult).then_inc(b_p, 1)

            def finish(g):
                need(pool, b_pr, g.n + 1)
                xg = X[:, g.buf8].rearrange("p (k d) -> p k d", d=D)
                G.tensor_tensor(xg, xg, q[:, g.buf2, :, 0:D], ALU.add).then_inc(b_fin, 1)

            def body_b(i):
                for r in range(U):
                    g, before = Group(i, r), Group(i, r - 1)
                    one, two = Group(i, r + 1), Group(i, r + 2)
                    for k in range(NT):
                        gather(g, k)
                        if before.exists():
                            if k == 3:
                                products(before)
                            if k == 10:
                                finish(before)
                        if one.exists() and k == 6:
                            low_half(one)
                        if two.exists() and k == 13:
                            inverse_deviation(two)

            pool.wait_ge(tab_out, 16)
            inverse_deviation(Group(0, 0))
            low_half(Group(0, 0))
            inverse_deviation(Group(0, 1))
            body_b(0)
            with pool.Fori(1, NI - 1) as i:
                body_b(i)
            body_b(NI - 1)
            products(Group(NI - 1, U - 1))
            finish(Group(NI - 1, U - 1))


def shape_constants():
    def cosines(freq, pos, n, weight_of):
        ends = (weight_of == 0) | (weight_of == n - 1)
        return np.cos(np.pi * np.multiply.outer(pos, freq) / (n - 1)) * np.where(ends, 1.0, 2.0)

    kx = np.concatenate([np.arange(MX // 2), np.arange(H - MX // 2, H)])
    ky = np.arange(MY)
    h, w = np.arange(H), np.arange(W)
    fh = cosines(kx, h, H, h[:, None]).reshape(P, T2, MX)
    fw = cosines(ky, w, W, w[:, None]).reshape(2, P, MY).transpose(1, 0, 2)
    ih = cosines(kx, h, H, kx[None, :]).reshape(P, T2, MX).transpose(2, 1, 0).reshape(MX, T2 * P)
    iw = np.tile(cosines(ky, w, W, ky[None, :]).T, (CG, 1))
    gm = (np.arange(P)[:, None] % C) // CG == np.arange(C // CG)[None, :]
    rm = np.arange(P)[:, None] == D + np.arange(3)[None, :]
    return [np.ascontiguousarray(a, dtype=np.float32) for a in (fh, fw, ih, iw, np.eye(P), gm, rm)]


def kernel(x, L0_conv_weights1, L0_conv_weights2, L1_conv_embeddings):
    import concourse.bacc as bacc
    from concourse.bass_utils import run_bass_kernel_spmd

    nc = bacc.Bacc("TRN2", target_bir_lowering=False, num_devices=1)
    given = [x, L0_conv_weights1, L0_conv_weights2, L1_conv_embeddings] + shape_constants()
    names = ["x", "w1", "w2", "emb", "c_fh", "c_fw", "c_ih", "c_iw", "c_id", "c_gm", "c_rm"]
    arrays = {n: np.ascontiguousarray(a) for n, a in zip(names, given)}
    args = [nc.dram_tensor(n, a.shape, F32, kind="ExternalInput").ap() for n, a in arrays.items()]
    args.append(nc.dram_tensor("y", (B, C, H, W), F32, kind="ExternalOutput").ap())
    program(nc, *args)
    return run_bass_kernel_spmd(nc, [arrays], core_ids=[0]).results[0]["y"]
```
